# Optimizing a Trainium2 kernel written in Bass

```python
import numpy as np
import jax
import jax.numpy as jnp

def _softmax(x, axis=-1):
    return jax.nn.softmax(x, axis=axis)

def _gelu(x):
    return jax.nn.gelu(x, approximate=True)

def _silu(x):
    return jax.nn.silu(x)

def _sigmoid(x):
    return jax.nn.sigmoid(x)

def _layernorm(x, axis=-1, eps=1e-05):
    m = jnp.mean(x, axis=axis, keepdims=True)
    v = jnp.var(x, axis=axis, keepdims=True)
    return (x - m) / jnp.sqrt(v + eps)

def _scatter_add(tgt, idx, src, axis=0):
    return tgt.at[idx].add(src)

def _segment_sum(src, seg, n):
    return jax.ops.segment_sum(src, seg, n)
kernel_name = 'mk_sandwich_d1_jaxref_r4_d14649'

def setup_inputs(seed: int=0):
    np.random.seed(seed)
    _w = jnp.asarray

    def _L0_attn_setup():
        import jax, jax.numpy as jnp
        import numpy as np
        D_MODEL = 256
        N_HEADS = 16
        D_K = D_MODEL // N_HEADS
        THETA = 10000.0
        MAX_SEQ = 512

        def _trunc_normal(key, shape, std):
            return jnp.clip(jax.random.normal(key, shape) * std, -3 * std, 3 * std).astype(jnp.float32)

        def _rope(x, positions):
            d = x.shape[-1]
            inv_freq = THETA ** (-2.0 * jnp.arange(0, d // 2, dtype=jnp.float32) / d)
            angles = positions.astype(jnp.float32)[:, None] * inv_freq[None, :]
            cos, sin = (jnp.cos(angles), jnp.sin(angles))
            xp = x.reshape(x.shape[:-1] + (d // 2, 2))
            x_even, x_odd = (xp[..., 0], xp[..., 1])
            out_even = x_even * cos - x_odd * sin
            out_odd = x_even * sin + x_odd * cos
            return jnp.stack((out_even, out_odd), axis=-1).reshape(x.shape)
        key = jax.random.key(seed)
        kx, kq, kk, kv, ko = jax.random.split(key, 5)
        std = np.sqrt(2.0 / (D_MODEL + D_MODEL))
        x = jax.random.normal(kx, (2, 512, D_MODEL), dtype=jnp.float32)
        W_q = _trunc_normal(kq, (D_MODEL, D_MODEL), std)
        W_k = _trunc_normal(kk, (D_MODEL, D_MODEL), std)
        W_v = _trunc_normal(kv, (D_MODEL, D_MODEL), std)
        W_o = _trunc_normal(ko, (D_MODEL, D_MODEL), std)
        return {'x': x, 'W_q': W_q, 'W_k': W_k, 'W_v': W_v, 'W_o': W_o}
    _L0_attn_in = _L0_attn_setup()

    def _L0_ffn_setup():
        import jax, jax.numpy as jnp
        import numpy as np
        E = 16
        K = 4
        NG = 4
        TG = 2
        SCALE = 2.5
        NORM_TOPK = True
        H = 256
        I = 128
        SH_I = I * 2
        B, S = (2, 512)
        key = jax.random.key(seed)
        ks = jax.random.split(key, 9)

        def w(k, shape, fan_in):
            return jax.random.normal(k, shape, jnp.float32) * (1.0 / np.sqrt(fan_in))
        return {'hidden_states': jax.random.normal(ks[0], (B, S, H), jnp.float32), 'gate_w': w(ks[1], (E, H), H), 'gate_bias': jnp.zeros((E,), jnp.float32), 'Wg': w(ks[2], (E, I, H), H), 'Wu': w(ks[3], (E, I, H), H), 'Wd': w(ks[4], (E, H, I), I), 'Ws_g': w(ks[5], (SH_I, H), H), 'Ws_u': w(ks[6], (SH_I, H), H), 'Ws_d': w(ks[7], (H, SH_I), SH_I)}
    _L0_ffn_in = _L0_ffn_setup()
    _d = {'L0_attn_x': _L0_attn_in['x'], 'L0_attn_W_q': _L0_attn_in['W_q'], 'L0_attn_W_k': _L0_attn_in['W_k'], 'L0_attn_W_v': _L0_attn_in['W_v'], 'L0_attn_W_o': _L0_attn_in['W_o'], 'L0_ffn_gate_w': _L0_ffn_in['gate_w'], 'L0_ffn_gate_bias': _L0_ffn_in['gate_bias'], 'L0_ffn_Wg': _L0_ffn_in['Wg'], 'L0_ffn_Wu': _L0_ffn_in['Wu'], 'L0_ffn_Wd': _L0_ffn_in['Wd'], 'L0_ffn_Ws_g': _L0_ffn_in['Ws_g'], 'L0_ffn_Ws_u': _L0_ffn_in['Ws_u'], 'L0_ffn_Ws_d': _L0_ffn_in['Ws_d']}
    _x0 = _d['L0_attn_x']
    _d['L0_attn_x'] = jax.random.normal(jax.random.fold_in(jax.random.key(seed), 1), (8, 512, 256), dtype=_x0.dtype)
    del _x0
    return _d

def reference(L0_attn_x, L0_attn_W_q, L0_attn_W_k, L0_attn_W_v, L0_attn_W_o, L0_ffn_gate_w, L0_ffn_gate_bias, L0_ffn_Wg, L0_ffn_Wu, L0_ffn_Wd, L0_ffn_Ws_g, L0_ffn_Ws_u, L0_ffn_Ws_d):

    def _L0_attn_ref(x, W_q, W_k, W_v, W_o):
        import jax, jax.numpy as jnp
        import numpy as np
        D_MODEL = 256
        N_HEADS = 16
        D_K = D_MODEL // N_HEADS
        THETA = 10000.0
        MAX_SEQ = 512

        def _trunc_normal(key, shape, std):
            return jnp.clip(jax.random.normal(key, shape) * std, -3 * std, 3 * std).astype(jnp.float32)

        def _rope(x, positions):
            d = x.shape[-1]
            inv_freq = THETA ** (-2.0 * jnp.arange(0, d // 2, dtype=jnp.float32) / d)
            angles = positions.astype(jnp.float32)[:, None] * inv_freq[None, :]
            cos, sin = (jnp.cos(angles), jnp.sin(angles))
            xp = x.reshape(x.shape[:-1] + (d // 2, 2))
            x_even, x_odd = (xp[..., 0], xp[..., 1])
            out_even = x_even * cos - x_odd * sin
            out_odd = x_even * sin + x_odd * cos
            return jnp.stack((out_even, out_odd), axis=-1).reshape(x.shape)
        b, s, _ = x.shape

        def split_heads(t):
            return t.reshape(b, s, N_HEADS, D_K).transpose(0, 2, 1, 3)
        Q = split_heads(x @ W_q.T)
        K = split_heads(x @ W_k.T)
        V = split_heads(x @ W_v.T)
        pos = jnp.arange(s)
        Q = _rope(Q, pos)
        K = _rope(K, pos)
        score = jnp.einsum('bnqd,bnkd->bnqk', Q, K) / jnp.sqrt(jnp.float32(D_K))
        causal = jnp.triu(jnp.ones((s, s), dtype=bool), k=1)
        score = jnp.where(causal[None, None], -jnp.inf, score)
        attn = jax.nn.softmax(score, axis=-1)
        out = jnp.einsum('bnqk,bnkd->bnqd', attn, V)
        out = out.transpose(0, 2, 1, 3).reshape(b, s, D_MODEL)
        return out @ W_o.T

    def _L0_ffn_ref(hidden_states, gate_w, gate_bias, Wg, Wu, Wd, Ws_g, Ws_u, Ws_d):
        import jax, jax.numpy as jnp
        import numpy as np
        E = 16
        K = 4
        NG = 4
        TG = 2
        SCALE = 2.5
        NORM_TOPK = True
        H = 256
        I = 128
        SH_I = I * 2
        B, S = (2, 512)
        x = hidden_states
        b, s, h = x.shape
        n = b * s
        xf = x.reshape(n, h)
        logits = xf @ gate_w.T
        scores = jax.nn.sigmoid(logits)
        sfc = scores + gate_bias
        epg = E // NG
        grp = sfc.reshape(n, NG, epg)
        g_scores = jax.lax.top_k(grp, 2)[0].sum(-1)
        _, gidx = jax.lax.top_k(g_scores, TG)
        gmask = jax.nn.one_hot(gidx, NG, dtype=sfc.dtype).sum(1)
        emask = jnp.repeat(gmask, epg, axis=1)
        masked = jnp.where(emask > 0, sfc, -jnp.inf)
        _, topk_idx = jax.lax.top_k(masked, K)
        topk_w = jnp.take_along_axis(scores, topk_idx, axis=1)
        if K > 1 and NORM_TOPK:
            topk_w = topk_w / (topk_w.sum(-1, keepdims=True) + 1e-20)
        topk_w = topk_w * SCALE
        cw = (jax.nn.one_hot(topk_idx, E, dtype=topk_w.dtype) * topk_w[..., None]).sum(1)
        hg = jnp.einsum('nh,eih->nei', xf, Wg)
        hu = jnp.einsum('nh,eih->nei', xf, Wu)
        act = jax.nn.silu(hg) * hu
        y = jnp.einsum('nei,ne,ehi->nh', act, cw, Wd)
        shared = jax.nn.silu(xf @ Ws_g.T) * (xf @ Ws_u.T) @ Ws_d.T
        y = y + shared
        return (x + y.reshape(b, s, h)).astype(hidden_states.dtype)
    x = L0_attn_x
    x = x + _layernorm(_L0_attn_ref(_layernorm(x, axis=-1), L0_attn_W_q, L0_attn_W_k, L0_attn_W_v, L0_attn_W_o), axis=-1)
    x = x + _layernorm(_L0_ffn_ref(_layernorm(x, axis=-1), L0_ffn_gate_w, L0_ffn_gate_bias, L0_ffn_Wg, L0_ffn_Wu, L0_ffn_Wd, L0_ffn_Ws_g, L0_ffn_Ws_u, L0_ffn_Ws_d), axis=-1)
    return x

_drawn_inputs = setup_inputs


def setup_inputs(seed=0):
    import zlib

    import numpy as np

    out = dict(_drawn_inputs(seed))
    spreads = {'L0_ffn_gate_bias': (0.0, 0.1)}
    factors = {}
    for name, (base, spread) in spreads.items():
        noise = np.random.default_rng([zlib.crc32(name.encode()), seed]).standard_normal(out[name].shape)
        drawn = base * np.exp(spread * noise) if base else spread * noise
        out[name] = jnp.asarray(drawn.astype(out[name].dtype))
    for name, factor in factors.items():
        out[name] = (out[name] * factor).astype(out[name].dtype)
    return out
```

```python
import numpy as np
import concourse.bass as bass
from concourse import mybir
from contextlib import ExitStack

B, T, D = 8, 512, 256
P = 128
NT = T // P
KD = D // P
H, DH = 16, 16
HALF = DH // 2
QUADS, PAIRS = H // 4, H // 2
E, FI, TOPK, NG = 16, 128, 4, 4
EPG = E // NG
SHARED = 2
UNITS = SHARED + E
EPS = 1e-5
ROUTE_SCALE = 2.5
SCALE = DH ** -0.5
MASKED = -1e38
BIG = 1e30

Q_PART = [0, 0, 0, 1, 1, 2]
K_PART = [0, 1, 2, 0, 1, 0]
SLOTS = len(Q_PART)
ROWS = SLOTS * DH
MROWS = ROWS + 3

C_QKV = 0
C_O = C_QKV + KD * 3 * D
C_SG = C_O + KD * D
C_SU = C_SG + KD * D
C_SD = C_SU + KD * D
C_GATE = C_SD + KD * D
C_ALL = C_GATE + KD * E
EXP_COLS = KD * FI * 2 + D

N_S = PAIRS * NT
N_ST = QUADS * NT * 2
N_AV = QUADS * NT
N_STACK = 2 * 2 * SLOTS


def attention_plan():
    plan = [("S", 0, qb) for qb in range(NT)] + [("S", 1, qb) for qb in range(NT)]
    plan += [("S", 2, qb) for qb in range(NT)][:2] + [("MT", 0)] + [("S", 2, qb) for qb in range(NT)][2:]
    s_rest = [("S", p, qb) for p in range(3, PAIRS) for qb in range(NT)]
    for q in range(QUADS):
        for kb in range(NT):
            for half in range(2):
                plan.append(("ST", q, kb, half))
                if s_rest:
                    plan.append(s_rest.pop(0))
            if kb >= 1:
                plan.append(("AV", q, kb - 1))
            elif q >= 1:
                plan += [("AV", q - 1, NT - 1)]
            if kb == 1 and q >= 1:
                plan.append(("OT", q - 1))
            if kb == 2 and q + 1 < QUADS:
                plan.append(("MT", q + 1))
        if q == 1:
            plan.append(("XT",))
    plan += [("AV", QUADS - 1, NT - 1), ("OT", QUADS - 1)]
    return plan


PLAN = attention_plan()


def block_kernel(nc, x, w_small, w_exp, rope, ties, bias, out):
    fp32, fp32r, bf16 = mybir.dt.float32, mybir.dt.float32r, mybir.dt.bfloat16
    ALU, ACT, AX = mybir.AluOpType, mybir.ActivationFunctionType, mybir.AxisListType

    ctx = ExitStack()
    with ctx:
        def sb(name, shape, dt=fp32):
            return ctx.enter_context(nc.sbuf_tensor(name, shape, dt))

        def sem(name):
            return ctx.enter_context(nc.semaphore(name))

        part_dram = nc.dram_tensor("part_scratch", (4, P, 3, T), bf16, kind="Internal").ap()
        cw_dram = nc.dram_tensor("cw_scratch", (E, T), fp32, kind="Internal").ap()

        w_hi = sb("w_hi", [P, C_ALL], fp32r)
        w_lo = sb("w_lo", [P, C_ALL], fp32r)
        w_raw = sb("w_raw", [P, E * EXP_COLS])
        gu_hi = sb("gu_hi", [P, 2, 2 * KD * FI], fp32r)
        gu_lo = sb("gu_lo", [P, 2, 2 * KD * FI], fp32r)
        dn_hi = sb("dn_hi", [P, 3, D], fp32r)
        dn_lo = sb("dn_lo", [P, 3, D], fp32r)
        rope_t = sb("rope_t", [P, 2, T])
        tie_t = sb("tie_t", [P, E * E + NG * NG])
        bias_t = sb("bias_t", [P, NT * E])
        ident = sb("ident", [P, P])
        ident_b = sb("ident_b", [P, P], bf16)
        mask_f = sb("mask_f", [P, P])
        mask_b = sb("mask_b", [P, P], bf16)
        minus_half = sb("minus_half", [P, NT])
        x_ln = sb("x_ln", [P, NT, D])
        xn = x_ln
        st1 = sb("st1", [P, NT, 6])
        mv1 = sb("mv1", [P, NT, 2])
        ve1 = sb("ve1", [P, NT])
        rstd1 = sb("rstd1", [P, NT])
        xt_hi = sb("xt_hi", [P, KD, T], fp32r)
        xt_lo = sb("xt_lo", [P, KD, T], fp32r)
        rot = sb("rot", [P, 4, T])
        part = sb("part", [P, 2, 2, 3, T], bf16)
        q_st = sb("q_st", [P, H, T], bf16)
        k_st = sb("k_st", [P, H, T], bf16)
        v_sb = sb("v_sb", [P, NT, H, 32])
        nmax = sb("nmax", [P, NT, H])
        mres = sb("mres", [P, 2, NT, 4])
        mpart = sb("mpart", [P, NT, 3, 4], bf16)
        mrow = sb("mrow", [12, T], bf16)
        prob = sb("prob", [P, 2, 4, T])
        o_t = sb("o_t", [P, T])
        rden = sb("rden", [P, NT, 4])
        ht_hi = sb("ht_hi", [P, KD, T], fp32r)
        ht_lo = sb("ht_lo", [P, KD, T], fp32r)
        x1 = sb("x1", [P, NT, D])
        xn2 = sb("xn2", [P, NT, D])
        att = xn2
        st2 = sb("st2", [P, NT, 6])
        mv2 = sb("mv2", [P, NT, 2])
        ve2 = sb("ve2", [P, NT])
        rstd2 = sb("rstd2", [P, NT])
        r_sc = sb("r_sc", [P, NT * E])
        r_sf = sb("r_sf", [P, NT * E])
        r_hi = sb("r_hi", [P, NT * NG, 2])
        r_lo = sb("r_lo", [P, NT * NG, 2])
        r_g = sb("r_g", [P, 5, NT * NG])
        r_b = prob[:, 0, 0:2, :].rearrange("p a n -> p (a n)")
        r_c = prob[:, 0, 2:4, :].rearrange("p a n -> p (a n)")
        r_d = sb("r_d", [P, 2, NT * E])
        cw = sb("cw", [P, NT, E])
        r_s = sb("r_s", [P, 3, NT])
        cw_t = o_t[0:E, :]
        cwb, silu, act = prob[:, 0, :, :], prob[:, 1, 0:2, :], prob[:, 1, 2:4, :]
        a_hi, a_lo = xt_hi, xt_lo
        stage = q_st[:, :, :].rearrange("p h n -> p (h n)").bitcast(fp32)[:, 0:C_ALL]

        ring = [ctx.enter_context(nc.psum_tensor(f"ring{i}", [P, 2, T], fp32)) for i in range(4)]
        O_BANK, M_BANK = ring[3][:, 0, :], ring[3][:, 1, :]
        m_bf = M_BANK.bitcast(bf16)

        s_small = sem("small_loaded")
        s_const = sem("constants_loaded")
        s_wexp = sem("experts_loaded")
        s_pool0 = sem("pool_constants")
        s_dve0 = sem("dve_constants")
        s_whi = sem("weights_high")
        s_wlo = sem("weights_low")
        s_seen_dve = sem("waited_dve")
        s_seen_pool = sem("waited_pool")
        s_x = sem("x_loaded")
        s_stat1 = sem("stats1")
        s_pow1 = sem("rstd1_ready")
        s_xn = sem("xn_ready")
        s_xnT = sem("xn_transposed")
        s_xthi = sem("xt_high")
        s_xtlo = sem("xt_low")
        s_qk = sem("qk_products")
        s_v = sem("v_products")
        s_vsb = sem("v_copied")
        s_rot = sem("rotary_products")
        s_sum = sem("rotary_sums")
        s_phi = sem("part_high")
        s_pres = sem("part_residual")
        s_pmid = sem("part_middle")
        s_plo = sem("part_low")
        s_pout = [sem(f"parts_stored{n}") for n in range(4)]
        s_stack = sem("stacked")
        s_S = sem("scores")
        s_max = sem("row_maxima")
        s_mp = sem("maxima_split")
        s_mT = sem("maxima_transposed")
        s_mrow = sem("maxima_rows")
        s_mdma = sem("maxima_stacked")
        s_ST = sem("scores_transposed")
        s_exp = sem("exponentials")
        s_tri = sem("diagonal_cut")
        s_av = sem("pv_step")
        s_o = sem("o_copied")
        s_oT = sem("o_transposed")
        s_rden = sem("denominators")
        s_att = sem("attention_rows")
        s_aT = sem("attention_transposed")
        s_athi = sem("at_high")
        s_atlo = sem("at_low")
        s_op = sem("o_projected")
        s_x1in = sem("x1_loaded")
        s_ln = sem("ln_steps")
        s_lnv = sem("ln_variance")
        s_lnr = sem("ln_rstd")
        s_xn2 = sem("xn2_ready")
        s_hT = sem("xn2_transposed")
        s_hthi = sem("ht_high")
        s_htlo = sem("ht_low")
        s_logit = sem("logits")
        s_score = sem("router_scores")
        s_route = sem("router_steps")
        s_cw = sem("gates_ready")
        s_cwT = sem("gates_transposed")
        s_cwrow = sem("gates_rows")
        s_cwout = sem("gates_stored")
        s_cwb = [sem(f"gates_broadcast{i}") for i in range(4)]
        s_whs = sem("expert_high")
        s_wls = sem("expert_low")
        s_gu = sem("gate_up")
        s_silu = sem("silu")
        s_t = sem("silu_times_up")
        s_a = sem("gated")
        s_ahi = sem("act_high")
        s_alo = sem("act_low")
        s_d = sem("down")
        s_y = sem("y_read")
        s_fln = sem("final_ln_steps")
        s_fv = sem("final_variance")
        s_fr = sem("final_rstd")
        s_out = sem("out_stored")

        def at(b, per_seq, n):
            return b * per_seq + n

        def seq(b):
            return bass.ds(b, 1) if not isinstance(b, int) else slice(b, b + 1)

        block = ctx.enter_context(nc.Block())

        @block.sync
        def _(sp):
            sp.dma_start(stage, w_small).then_inc(s_small, 16)

            def load_x(b, first=False):
                if not first:
                    sp.wait_ge(s_xnT, b)
                sp.dma_start(x_ln[:, :, :], x[seq(b)].rearrange("a (t p) d -> p (a t) d", p=P)).then_inc(s_x, 16)

            def load_x1(b):
                sp.dma_start(x1[:, :, :], x[seq(b)].rearrange("a (t p) d -> p (a t) d", p=P)).then_inc(s_x1in, 16)

            def stack(b, first=False):
                if first:
                    sp.wait_ge(s_wlo, 1)
                else:
                    sp.wait_ge(s_ST, b * N_ST)
                for n in range(4):
                    sp.wait_ge(s_plo, at(b, 4, n + 1))
                    sp.dma_start(part_dram[n], part[:, n // 2, n % 2, :, :]).then_inc(s_pout[n], 16)
                for n in range(4):
                    dst, parts = ((q_st, Q_PART), (k_st, K_PART))[n // 2]
                    sp.wait_ge(s_pout[n], at(b, 16, 16))
                    for s in range(SLOTS):
                        r = s * DH + (n % 2) * HALF
                        by_pair = part_dram[n, :, parts[s], :].rearrange("(h j) t -> j h t", j=HALF)
                        sp.dma_start(dst[r:r + HALF, :, :], by_pair).then_inc(s_stack, 16)

            def attend(b):
                for q in range(QUADS):
                    sp.wait_ge(s_mrow, at(b, QUADS, q + 1))
                    sp.dma_start(q_st[ROWS:MROWS, 4 * q:4 * q + 4, :],
                                 mrow[:, :]).then_inc(s_mdma, 16)

            def ffn(b, last=False):
                sp.wait_ge(s_cwrow, at(b, 1, 1))
                sp.dma_start(cw_dram, cw_t[:, :]).then_inc(s_cwout, 16)
                sp.wait_ge(s_cwout, at(b, 16, 16))
                for e in range(E):
                    if e >= 4:
                        sp.wait_ge(s_a, at(b, E, e - 3))
                    sp.dma_start(cwb[:, e % 4, :], cw_dram[e:e + 1, :].to_broadcast([P, T])).then_inc(s_cwb[e % 4], 16)
                sp.wait_ge(s_fln, at(b, FLN, FLN))
                sp.dma_start(out[seq(b)].rearrange("a (t p) d -> p (a t) d", p=P), xn2[:, :, :]).then_inc(s_out, 16)
                sp.wait_ge(s_out, at(b, 16, 16))

            load_x(0, first=True)
            sp.dma_start(rope_t[:, :, :], rope).then_inc(s_const, 16)
            sp.dma_start(tie_t[:, :], ties).then_inc(s_const, 16)
            sp.dma_start(bias_t[:, :], bias).then_inc(s_const, 16)
            load_x1(0)
            for e in range(0, E, 4):
                sp.dma_start(w_raw[:, e * EXP_COLS:(e + 4) * EXP_COLS], w_exp[:, e * EXP_COLS:(e + 4) * EXP_COLS]
                             ).then_inc(s_wexp, 16)
            stack(0, first=True)
            with sp.Fori(0, B - 1) as i:
                load_x(i + 1)
                attend(i)
                stack(i + 1)
                ffn(i)
                load_x1(i + 1)
            attend(B - 1)
            ffn(B - 1, last=True)

        @block.gpsimd
        def _(pool):
            pool.memset(ident[:, :], 0.0).then_inc(s_pool0, 1)
            pool.memset(mask_f[:, :], 0.0).then_inc(s_pool0, 1)
            pool.memset(minus_half[:, :], -0.5).then_inc(s_pool0, 1)
            pool.memset(v_sb[:, :, :, :], 0.0).then_inc(s_pool0, 1)
            pool.memset(k_st[:, :, :], 1.0).then_inc(s_pool0, 1)
            pool.wait_ge(s_pool0, 5)
            pool.affine_select(out=ident[:, :], in_=ident[:, :], compare_op=ALU.not_equal, fill=1.0,
                               base=0, pattern=[[-1, P]], channel_multiplier=1).then_inc(s_pool0, 1)
            pool.affine_select(out=mask_f[:, :], in_=mask_f[:, :], compare_op=ALU.is_ge, fill=MASKED,
                               base=0, pattern=[[-1, P]], channel_multiplier=1).then_inc(s_pool0, 1)
            pool.memset(v_sb[:, :, :, DH:DH + 1], 1.0).then_inc(s_pool0, 1)

            def norm(b):
                pool.wait_ge(s_stat1, at(b, N_STAT, N_STAT))
                pool.tensor_tensor(rstd1[:, :], ve1[:, :], minus_half[:, :], ALU.pow).then_inc(s_pow1, 1)

            def project(b):
                for qk in range(2):
                    pool.wait_ge(s_rot, at(b, 8, 4 * qk + 4))
                    pool.tensor_tensor(rot[:, 0, :], rot[:, 0, :], rot[:, 1, :], ALU.subtract).then_inc(s_sum, 1)
                    pool.tensor_tensor(rot[:, 2, :], rot[:, 2, :], rot[:, 3, :], ALU.add).then_inc(s_sum, 1)

            def attend(b):
                for u in range(N_AV):
                    pool.wait_ge(s_exp, at(b, N_ST, 2 * u + 2))
                    pool.sem_inc(s_seen_pool, 1)
                    diag = prob[:, u % 2, :, 0:P]
                    pool.affine_select(out=diag, in_=diag, compare_op=ALU.is_ge, fill=0.0, base=0,
                                       pattern=[[0, 4], [1, P]], channel_multiplier=-1).then_inc(s_tri, 1)
                for n in range(2):
                    pool.wait_ge(s_lnv, at(b, 2, n + 1))
                    pool.tensor_tensor(rstd2[:, :], ve2[:, :], minus_half[:, :], ALU.pow).then_inc(s_lnr, 1)

            def ffn(b):
                for u in range(SHARED, UNITS):
                    e = u - SHARED
                    pool.wait_ge(s_whs, at(b, E, e + 1))
                    raw = w_raw[:, e * EXP_COLS:(e + 1) * EXP_COLS]
                    gu = 2 * KD * FI
                    pool.tensor_tensor(gu_lo[:, u % 2, :], raw[:, 0:gu], gu_hi[:, u % 2, :], ALU.subtract)
                    pool.tensor_tensor(dn_lo[:, u % 3, :], raw[:, gu:], dn_hi[:, u % 3, :],
                                       ALU.subtract).then_inc(s_wls, 1)
                pool.wait_ge(s_fv, at(b, 1, 1))
                pool.tensor_tensor(rstd2[:, :], ve2[:, :], minus_half[:, :], ALU.pow).then_inc(s_fr, 1)

            norm(0)
            project(0)
            with pool.Fori(0, B - 1) as i:
                norm(i + 1)
                attend(i)
                project(i + 1)
                ffn(i)
            attend(B - 1)
            ffn(B - 1)

        @block.vector
        def _(dve):
            dve.wait_ge(s_pool0, 8)
            dve.tensor_copy(ident_b[:, :], ident[:, :]).then_inc(s_dve0, 1)
            dve.tensor_copy(mask_b[:, :], mask_f[:, :]).then_inc(s_dve0, 1)
            dve.wait_ge(s_whi, 1)
            dve.tensor_tensor(w_lo[:, :], stage, w_hi[:, :], ALU.subtract).then_inc(s_wlo, 1)

            def norm(b, first=False):
                dve.wait_ge(s_x, at(b, 16, 16))
                for t in range(NT):
                    dve.bn_stats(st1[:, t, :], x_ln[:, t, :]).then_inc(s_stat1, 1)
                for t in range(NT):
                    dve.wait_ge(s_stat1, at(b, N_STAT, t + 1))
                    dve.sem_inc(s_seen_dve, 1)
                    dve.bn_aggr(mv1[:, t, :], st1[:, t, :]).then_inc(s_stat1, 1)
                dve.wait_ge(s_stat1, at(b, N_STAT, 2 * NT))
                dve.tensor_scalar(ve1[:, :], mv1[:, :, 1], EPS, None, ALU.add).then_inc(s_stat1, 1)
                dve.wait_ge(s_pow1, at(b, 1, 1))
                for t in range(NT):
                    dve.tensor_scalar(xn[:, t, :], x_ln[:, t, :], mv1[:, t, 0:1], rstd1[:, t:t + 1],
                                      ALU.subtract, ALU.mult).then_inc(s_xn, 1)

            def xt_low(b, slot):
                dve.wait_ge(s_xthi, at(b, 1, 1))
                dve.tensor_tensor(xt_lo[:, :, :], slot[:, :, :], xt_hi[:, :, :], ALU.subtract).then_inc(s_xtlo, 1)

            def project(b, first=False):
                if first:
                    dve.wait_ge(s_const, 48)
                else:
                    dve.wait_ge(s_stack, b * N_STACK * 16)
                cos, sin = rope_t[:, 0, :], rope_t[:, 1, :]
                for qk in range(2):
                    dve.wait_ge(s_qk, at(b, 2, qk + 1))
                    if qk:
                        dve.wait_ge(s_plo, at(b, 4, 2))
                    even, odd = ring[1 + qk][:, 0, :], ring[1 + qk][:, 1, :]
                    for n, (src, tab) in enumerate(((even, cos), (odd, sin), (even, sin), (odd, cos))):
                        dve.tensor_tensor(rot[:, n, :], src, tab, ALU.mult).then_inc(s_rot, 1)
                    for eo in range(2):
                        n, full = 2 * qk + eo, rot[:, 2 * eo, :]
                        dve.wait_ge(s_phi, at(b, 4, n + 1))
                        dve.tensor_tensor(rot[:, 2 * eo + 1, :], full, part[:, qk, eo, 0, :],
                                          ALU.subtract).then_inc(s_pres, 1)
                        dve.wait_ge(s_pmid, at(b, 4, n + 1))
                        dve.tensor_tensor(part[:, qk, eo, 2, :], rot[:, 2 * eo + 1, :], part[:, qk, eo, 1, :],
                                          ALU.subtract).then_inc(s_plo, 1)

            def row_max(b, n_s, slot, pair, qb):
                dve.wait_ge(s_S, at(b, N_S, n_s + 1))
                n = (qb + 1) * P
                dve.tensor_reduce(nmax[:, qb, 2 * pair:2 * pair + 2], slot[:, :, 0:n], AX.X, ALU.max,
                                  negate=True).then_inc(s_max, 1)

            def split_max(b, q):
                full = nmax[:, :, 4 * q:4 * q + 4]
                dve.wait_ge(s_max, at(b, N_S, (2 * q + 2) * NT))
                if q:
                    dve.wait_ge(s_mT, at(b, QUADS, q))
                base = 5 * q
                dve.tensor_copy(mpart[:, :, 0, :], full).then_inc(s_mp, 1)
                dve.wait_ge(s_mp, at(b, 5 * QUADS, base + 1))
                dve.tensor_tensor(mres[:, 0, :, :], full, mpart[:, :, 0, :], ALU.subtract).then_inc(s_mp, 1)
                dve.wait_ge(s_mp, at(b, 5 * QUADS, base + 2))
                dve.tensor_copy(mpart[:, :, 1, :], mres[:, 0, :, :]).then_inc(s_mp, 1)
                dve.wait_ge(s_mp, at(b, 5 * QUADS, base + 3))
                dve.tensor_tensor(mres[:, 1, :, :], mres[:, 0, :, :], mpart[:, :, 1, :],
                                  ALU.subtract).then_inc(s_mp, 1)
                dve.wait_ge(s_mp, at(b, 5 * QUADS, base + 4))
                dve.tensor_copy(mpart[:, :, 2, :], mres[:, 1, :, :]).then_inc(s_mp, 1)

            def head_rows(b, q):
                o = M_BANK.rearrange("p (t h c) -> p t h c", t=NT, h=4)
                dve.wait_ge(s_oT, at(b, QUADS, q + 1))
                if q == 0:
                    dve.wait_ge(s_x1in, at(b, 16, 16))
                dve.reciprocal(rden[:, :, :], o[:, :, :, DH]).then_inc(s_rden, 1)
                dve.wait_ge(s_rden, at(b, QUADS, q + 1))
                dst = att[:, :, :].rearrange("p t (h c) -> p t h c", c=DH)[:, :, 4 * q:4 * q + 4, :]
                dve.tensor_tensor(dst, o[:, :, :, 0:DH], rden[:, :, :].unsqueeze(3).to_broadcast([P, NT, 4, DH]),
                                  ALU.mult).then_inc(s_att, 1)

            def statistics(src, step, value, v_sem, total, b):
                for t in range(NT):
                    dve.bn_stats(st2[:, t, :], src(t)).then_inc(step, 1)
                for t in range(NT):
                    dve.wait_ge(step, at(b, total, value + t + 1))
                    dve.sem_inc(s_seen_dve, 1)
                    dve.bn_aggr(mv2[:, t, :], st2[:, t, :]).then_inc(step, 1)
                dve.wait_ge(step, at(b, total, value + 2 * NT))
                dve.tensor_scalar(ve2[:, :], mv2[:, :, 1], EPS, None, ALU.add).then_inc(v_sem, 1)

            def attend(b, nxt):
                n_s = n = 0
                for step in PLAN:
                    if step[0] in ("S", "ST", "XT"):
                        slot = ring[(n + 1) % 3]
                        n += 1
                    if step[0] == "S":
                        row_max(b, n_s, slot, step[1], step[2])
                        n_s += 1
                    elif step[0] == "MT":
                        split_max(b, step[1])
                    elif step[0] == "OT":
                        head_rows(b, step[1])
                    elif step[0] == "XT" and nxt is not None:
                        xt_low(nxt, slot)
                dve.wait_ge(s_athi, at(b, 1, 1))
                dve.tensor_tensor(ht_lo[:, :, :], ring[0][:, :, :], ht_hi[:, :, :], ALU.subtract).then_inc(s_atlo, 1)
                proj = ring[0][:, :, :].rearrange("p a (c d) -> p (a c) d", d=D)
                dve.wait_ge(s_op, at(b, 1, 1))
                statistics(lambda t: proj[:, t, :], s_ln, 0, s_lnv, LN_STEPS, b)
                dve.wait_ge(s_lnr, at(b, 2, 1))
                for t in range(NT):
                    dve.tensor_scalar(xn2[:, t, :], proj[:, t, :], mv2[:, t, 0:1], rstd2[:, t:t + 1],
                                      ALU.subtract, ALU.mult).then_inc(s_ln, 1)
                for t in range(NT):
                    dve.wait_ge(s_ln, at(b, LN_STEPS, 2 * NT + t + 1))
                    dve.tensor_tensor(x1[:, t, :], x1[:, t, :], xn2[:, t, :], ALU.add).then_inc(s_ln, 1)
                dve.wait_ge(s_ln, at(b, LN_STEPS, 4 * NT))
                statistics(lambda t: x1[:, t, :], s_ln, 4 * NT, s_lnv, LN_STEPS, b)
                dve.wait_ge(s_lnr, at(b, 2, 2))
                for t in range(NT):
                    dve.tensor_scalar(xn2[:, t, :], x1[:, t, :], mv2[:, t, 0:1], rstd2[:, t:t + 1],
                                      ALU.subtract, ALU.mult).then_inc(s_xn2, 1)

            def route(b):
                count = [0]

                def step(ins):
                    count[0] += 1
                    ins.then_inc(s_route, 1)
                    dve.wait_ge(s_route, at(b, ROUTE_STEPS, count[0]))

                def beaten(rank, v, n, tie, wide_a, wide_b):
                    other = v.unsqueeze(2).to_broadcast([P, NT, n, n])
                    own = v.unsqueeze(3).to_broadcast([P, NT, n, n])
                    a = wide_a[:, 0:NT * n * n].rearrange("p (t g k) -> p t g k", t=NT, g=n)
                    c = wide_b[:, 0:NT * n * n].rearrange("p (t g k) -> p t g k", t=NT, g=n)
                    tb = tie.rearrange("p (g k) -> p g k", g=n).unsqueeze(1).to_broadcast([P, NT, n, n])
                    step(dve.tensor_tensor(a, other, own, ALU.is_equal))
                    step(dve.tensor_tensor(a, a, tb, ALU.mult))
                    step(dve.tensor_tensor(c, other, own, ALU.is_gt))
                    step(dve.tensor_tensor(a, a, c, ALU.add))
                    step(dve.tensor_reduce(rank, a, AX.X, ALU.add))

                t_e = lambda ap: ap.rearrange("p (t e) -> p t e", t=NT)
                t_g = lambda ap: ap.rearrange("p (t g) -> p t g", t=NT)
                grouped = lambda ap: ap.rearrange("p (g k) -> p g k", k=EPG)
                dve.wait_ge(s_score, at(b, 1, 1))
                step(dve.tensor_tensor(r_sf[:, :], r_sc[:, :], bias_t[:, :], ALU.add))
                quad = grouped(r_sf[:, :]).rearrange("p g (a c) -> p g a c", a=2)
                step(dve.tensor_tensor(r_hi[:, :, :], quad[:, :, :, 0], quad[:, :, :, 1], ALU.max))
                step(dve.tensor_tensor(r_lo[:, :, :], quad[:, :, :, 0], quad[:, :, :, 1], ALU.min))
                step(dve.tensor_tensor(r_g[:, 0, :], r_hi[:, :, 0], r_hi[:, :, 1], ALU.max))
                step(dve.tensor_tensor(r_g[:, 1, :], r_hi[:, :, 0], r_hi[:, :, 1], ALU.min))
                step(dve.tensor_tensor(r_g[:, 2, :], r_lo[:, :, 0], r_lo[:, :, 1], ALU.max))
                step(dve.tensor_tensor(r_g[:, 1, :], r_g[:, 1, :], r_g[:, 2, :], ALU.max))
                step(dve.tensor_tensor(r_g[:, 0, :], r_g[:, 0, :], r_g[:, 1, :], ALU.add))
                beaten(t_g(r_g[:, 3, :]), t_g(r_g[:, 0, :]), NG, tie_t[:, E * E:], r_b, r_c)
                step(dve.tensor_scalar(r_g[:, 3, :], r_g[:, 3, :], 1.5, None, ALU.is_lt))
                step(dve.tensor_scalar(r_g[:, 4, :], r_g[:, 3, :], BIG, -BIG, ALU.mult, ALU.add))
                wide = [P, NT * NG, EPG]
                step(dve.tensor_tensor(grouped(r_sf[:, :]), grouped(r_sf[:, :]),
                                       r_g[:, 3, :].unsqueeze(2).to_broadcast(wide), ALU.mult))
                step(dve.tensor_tensor(grouped(r_sf[:, :]), grouped(r_sf[:, :]),
                                       r_g[:, 4, :].unsqueeze(2).to_broadcast(wide), ALU.add))
                beaten(t_e(r_d[:, 0, :]), t_e(r_sf[:, :]), E, tie_t[:, 0:E * E], r_b, r_c)
                step(dve.tensor_scalar(r_d[:, 0, :], r_d[:, 0, :], TOPK - 0.5, None, ALU.is_lt))
                step(dve.tensor_tensor(r_d[:, 1, :], r_d[:, 0, :], r_sc[:, :], ALU.mult))
                step(dve.tensor_reduce(r_s[:, 0, :], t_e(r_d[:, 1, :]), AX.X, ALU.add))
                step(dve.tensor_scalar(r_s[:, 1, :], r_s[:, 0, :], 1e-20, None, ALU.add))
                step(dve.reciprocal(r_s[:, 2, :], r_s[:, 1, :]))
                step(dve.tensor_tensor(t_e(r_d[:, 1, :]), t_e(r_d[:, 1, :]),
                                       r_s[:, 2, :].unsqueeze(2).to_broadcast([P, NT, E]), ALU.mult))
                assert count[0] == ROUTE_STEPS
                dve.tensor_scalar(cw[:, :, :], t_e(r_d[:, 1, :]), ROUTE_SCALE, None, ALU.mult).then_inc(s_cw, 1)

            def ffn(b):
                dve.wait_ge(s_hthi, at(b, 1, 1))
                dve.tensor_tensor(ht_lo[:, :, :], ring[0][:, :, :], ht_hi[:, :, :], ALU.subtract).then_inc(s_htlo, 1)
                route(b)

                def low(u):
                    dve.wait_ge(s_ahi, at(b, UNITS, u + 1))
                    dve.tensor_tensor(a_lo[:, u % 2, :], act[:, u % 2, :], a_hi[:, u % 2, :],
                                      ALU.subtract).then_inc(s_alo, 1)

                for u in range(UNITS):
                    if u >= 2:
                        dve.wait_ge(s_alo, at(b, UNITS, u - 1))
                    dve.wait_ge(s_silu, at(b, UNITS, u + 1))
                    dve.tensor_tensor(act[:, u % 2, :], silu[:, u % 2, :], ring[1 + u % 3][:, 1, :],
                                      ALU.mult).then_inc(s_t, 1)
                    if u >= SHARED:
                        e = u - SHARED
                        dve.wait_ge(s_t, at(b, UNITS, u + 1))
                        dve.wait_ge(s_cwb[e % 4], at(b, 16 * (E // 4), 16 * (e // 4 + 1)))
                        dve.tensor_tensor(act[:, u % 2, :], act[:, u % 2, :], cwb[:, e % 4, :],
                                          ALU.mult).then_inc(s_a, 1)
                    if u >= 1:
                        low(u - 1)
                low(UNITS - 1)
                y = ring[0][:, :, :].rearrange("p a (c d) -> p (a c) d", d=D)
                dve.wait_ge(s_d, at(b, UNITS, UNITS))
                dve.tensor_tensor(xn2[:, :, :], y, xn2[:, :, :], ALU.add).then_inc(s_y, 1)
                dve.wait_ge(s_y, at(b, 1, 2))
                statistics(lambda t: xn2[:, t, :], s_fln, 0, s_fv, FLN, b)
                dve.wait_ge(s_fr, at(b, 1, 1))
                for t in range(NT):
                    dve.tensor_scalar(xn2[:, t, :], xn2[:, t, :], mv2[:, t, 0:1], rstd2[:, t:t + 1],
                                      ALU.subtract, ALU.mult).then_inc(s_fln, 1)
                for t in range(NT):
                    dve.wait_ge(s_fln, at(b, FLN, 2 * NT + t + 1))
                    dve.tensor_tensor(xn2[:, t, :], xn2[:, t, :], x1[:, t, :], ALU.add).then_inc(s_fln, 1)

            norm(0, first=True)
            xt_low(0, ring[0])
            dve.memset(r_s[:, :, :], 0.0).then_inc(s_y, 1)
            project(0, first=True)
            with dve.Fori(0, B - 1) as i:
                norm(i + 1)
                attend(i, i + 1)
                project(i + 1)
                ffn(i)
            attend(B - 1, None)
            ffn(B - 1)

        @block.scalar
        def _(act_e):
            act_e.wait_ge(s_small, 16)
            act_e.activation(w_hi[:, :], stage, ACT.Copy).then_inc(s_whi, 1)

            def xt_high(b, slot, first=False):
                act_e.wait_ge(s_xnT, at(b, 1, 1))
                if not first:
                    act_e.wait_ge(s_v, b)
                act_e.activation(xt_hi[:, :, :], slot[:, :, :], ACT.Copy).then_inc(s_xthi, 1)

            def project(b, first=False):
                if first:
                    act_e.wait_ge(s_pool0, 8)
                else:
                    act_e.wait_ge(s_av, b * N_AV)
                act_e.wait_ge(s_v, at(b, 1, 1))
                v = ring[0][:, :, :].rearrange("p a (c h d) -> p (a c) h d", c=2, h=H)
                for t in range(NT):
                    act_e.activation(v_sb[:, t, :, 0:DH], v[:, t, :, :], ACT.Copy).then_inc(s_vsb, 1)
                if not first:
                    act_e.wait_ge(s_stack, b * N_STACK * 16)
                for qk in range(2):
                    for eo in range(2):
                        n = 2 * qk + eo
                        act_e.wait_ge(s_sum, at(b, 4, n + 1))
                        act_e.activation(part[:, qk, eo, 0, :], rot[:, 2 * eo, :], ACT.Copy).then_inc(s_phi, 1)
                        act_e.wait_ge(s_pres, at(b, 4, n + 1))
                        act_e.activation(part[:, qk, eo, 1, :], rot[:, 2 * eo + 1, :], ACT.Copy).then_inc(s_pmid, 1)

            def attend(b, nxt):
                n = n_st = 0
                for step in PLAN:
                    if step[0] in ("S", "ST", "XT"):
                        slot = ring[(n + 1) % 3]
                        n += 1
                    if step[0] == "ST":
                        _, q, kb, half = step
                        u, width = q * NT + kb, T - kb * P
                        act_e.wait_ge(s_ST, at(b, N_ST, n_st + 1))
                        if u >= 2 and half == 0:
                            act_e.wait_ge(s_av, at(b, N_AV, u - 1))
                        act_e.activation(prob[:, u % 2, 2 * half:2 * half + 2, 0:width], slot[:, :, 0:width],
                                         ACT.Exp, scale=SCALE).then_inc(s_exp, 1)
                        n_st += 1
                    elif step[0] == "MT":
                        q = step[1]
                        act_e.wait_ge(s_mT, at(b, QUADS, q + 1))
                        if q:
                            act_e.wait_ge(s_mdma, at(b, 16 * QUADS, 16 * q))
                        act_e.activation(mrow[:, :], m_bf[0:12, 0:T], ACT.Copy).then_inc(s_mrow, 1)
                    elif step[0] == "AV" and step[2] == NT - 1:
                        q = step[1]
                        act_e.wait_ge(s_av, at(b, N_AV, (q + 1) * NT))
                        if q:
                            act_e.wait_ge(s_oT, at(b, QUADS, q))
                        act_e.activation(o_t[:, :], O_BANK, ACT.Copy).then_inc(s_o, 1)
                    elif step[0] == "XT" and nxt is not None:
                        xt_high(nxt, slot)
                act_e.wait_ge(s_aT, at(b, 1, 1))
                act_e.activation(ht_hi[:, :, :], ring[0][:, :, :], ACT.Copy).then_inc(s_athi, 1)

            def ffn(b):
                act_e.wait_ge(s_hT, at(b, 1, 1))
                act_e.activation(ht_hi[:, :, :], ring[0][:, :, :], ACT.Copy).then_inc(s_hthi, 1)
                act_e.wait_ge(s_logit, at(b, 1, 1))
                act_e.activation(r_sc[:, :], M_BANK[:, 0:NT * E], ACT.Sigmoid).then_inc(s_score, 1)

                def expert_high(u):
                    e = u - SHARED
                    act_e.wait_ge(s_gu, at(b, UNITS, max(1, u - 1) if u >= 4 else 1))
                    if u >= 5:
                        act_e.wait_ge(s_d, at(b, UNITS, u - 2))
                    raw = w_raw[:, e * EXP_COLS:(e + 1) * EXP_COLS]
                    gu = 2 * KD * FI
                    act_e.activation(gu_hi[:, u % 2, :], raw[:, 0:gu], ACT.Copy)
                    act_e.activation(dn_hi[:, u % 3, :], raw[:, gu:], ACT.Copy).then_inc(s_whs, 1)

                def silu_of(u):
                    act_e.wait_ge(s_gu, at(b, UNITS, u + 1))
                    if u >= 2:
                        act_e.wait_ge(s_t, at(b, UNITS, u - 1))
                    act_e.activation(silu[:, u % 2, :], ring[1 + u % 3][:, 0, :], ACT.Silu).then_inc(s_silu, 1)

                def high(u):
                    if u < SHARED:
                        act_e.wait_ge(s_t, at(b, UNITS, u + 1))
                    else:
                        act_e.wait_ge(s_a, at(b, E, u - SHARED + 1))
                    if u >= 2:
                        act_e.wait_ge(s_d, at(b, UNITS, u - 1))
                    act_e.activation(a_hi[:, u % 2, :], act[:, u % 2, :], ACT.Copy).then_inc(s_ahi, 1)

                act_e.wait_ge(s_wexp, 64)
                for u in range(UNITS):
                    silu_of(u)
                    if u >= 1:
                        high(u - 1)
                    if u == 1:
                        act_e.wait_ge(s_cwT, at(b, 1, 1))
                        act_e.activation(cw_t[:, :], ring[0][0:E, 0, :], ACT.Copy).then_inc(s_cwrow, 1)
                    if u == 0:
                        expert_high(SHARED)
                        expert_high(SHARED + 1)
                    elif u + 2 >= 4 and u + 2 < UNITS:
                        expert_high(u + 2)
                high(UNITS - 1)

            xt_high(0, ring[0], first=True)
            project(0, first=True)
            with act_e.Fori(0, B - 1) as i:
                attend(i, i + 1)
                project(i + 1)
                ffn(i)
            attend(B - 1, None)
            ffn(B - 1)

        @block.tensor
        def _(pe):
            pe.wait_ge(s_pool0, 8)
            pe.wait_ge(s_dve0, 2)

            def split_product(dst, l_hi, l_lo, r_hi, r_lo, start, stop, **kw):
                pe.matmul(dst, l_lo, r_hi, start=start, stop=False, **kw)
                pe.matmul(dst, l_hi, r_lo, start=False, stop=False, **kw)
                return pe.matmul(dst, l_hi, r_hi, start=False, stop=stop, **kw)

            def weight(tile, col, k, width, m, n):
                c = col + k * width + m
                return tile[:, c:c + n]

            def transpose_rows(slot, rows):
                for k in range(KD):
                    for t in range(NT):
                        last = pe.transpose(slot[:, k, t * P:(t + 1) * P], rows[:, t, k * P:(k + 1) * P], ident[:, :])
                return last

            def xt(b, slot):
                pe.wait_ge(s_xn, at(b, NT, NT))
                transpose_rows(slot, xn).then_inc(s_xnT, 1)

            def project(b, first=False):
                if first:
                    pe.wait_ge(s_wlo, 1)
                pe.wait_ge(s_xthi, at(b, 1, 1))
                pe.wait_ge(s_xtlo, at(b, 1, 1))
                for qk in range(2):
                    for eo in range(2):
                        m = (2 * qk + eo) * P
                        for k in range(KD):
                            last = split_product(ring[1 + qk][:, eo, :],
                                                 weight(w_hi, C_QKV, k, 3 * D, m, P), weight(w_lo, C_QKV, k, 3 * D, m, P),
                                                 xt_hi[:, k, :], xt_lo[:, k, :], k == 0, k == KD - 1)
                    last.then_inc(s_qk, 1)
                if not first:
                    pe.wait_ge(s_ln, at(b, LN_STEPS, 0) - (LN_STEPS - 3 * NT))
                for t in range(NT):
                    dst = ring[0][:, t // 2, (t % 2) * D:(t % 2 + 1) * D]
                    tok = slice(t * P, (t + 1) * P)
                    for k in range(KD):
                        last = split_product(dst, xt_hi[:, k, tok], xt_lo[:, k, tok],
                                             weight(w_hi, C_QKV, k, 3 * D, 2 * D, D),
                                             weight(w_lo, C_QKV, k, 3 * D, 2 * D, D), k == 0, k == KD - 1)
                last.then_inc(s_v, 1)

            def attend(b, nxt):
                pe.wait_ge(s_stack, at(b, N_STACK * 16, N_STACK * 16))
                n = n_s = n_st = 0
                user = [None] * 3
                user[0] = (s_y, at(b, 1, 1))
                m_user = None

                for step in PLAN:
                    kind = step[0]
                    if kind == "XT" and nxt is None:
                        n += 1
                        continue
                    if kind in ("S", "ST", "XT"):
                        r = (n + 1) % 3
                        slot = ring[r]
                        n += 1
                        if user[r] is not None:
                            pe.wait_ge(*user[r])
                    if kind == "S":
                        _, pair, qb = step
                        width, q0 = (qb + 1) * P, qb * P
                        for j in range(2):
                            h = 2 * pair + j
                            pe.matmul(slot[:, j, 0:width], q_st[0:ROWS, h, q0:q0 + P], k_st[0:ROWS, h, 0:width],
                                      start=True, stop=False)
                            last = pe.matmul(slot[:, j, q0:q0 + P], ident_b[:, :], mask_b[:, :], start=False, stop=True)
                        last.then_inc(s_S, 1)
                        n_s += 1
                        user[r] = (s_max, at(b, N_S, n_s))
                    elif kind == "ST":
                        _, q, kb, half = step
                        if kb == 0 and half == 0:
                            pe.wait_ge(s_mdma, at(b, 16 * QUADS, 16 * (q + 1)))
                        for j in range(2):
                            h = 4 * q + 2 * half + j
                            last = pe.matmul(slot[:, j, 0:T - kb * P], k_st[0:MROWS, h, kb * P:(kb + 1) * P],
                                             q_st[0:MROWS, h, kb * P:T], start=True, stop=True)
                        last.then_inc(s_ST, 1)
                        n_st += 1
                        user[r] = (s_exp, at(b, N_ST, n_st))
                    elif kind == "AV":
                        _, q, kb = step
                        u = q * NT + kb
                        pe.wait_ge(s_tri, at(b, N_AV, u + 1))
                        if kb == 0:
                            if u == 0:
                                pe.wait_ge(s_vsb, at(b, NT, NT))
                            else:
                                pe.wait_ge(s_o, at(b, QUADS, q))
                        for j in range(4):
                            last = pe.matmul(O_BANK[32 * j:32 * j + 32, kb * P:T], v_sb[:, kb, 4 * q + j, :],
                                             prob[:, u % 2, j, 0:T - kb * P], start=(kb == 0), stop=(kb == NT - 1))
                        last.then_inc(s_av, 1)
                    elif kind == "MT":
                        q = step[1]
                        pe.wait_ge(s_mp, at(b, 5 * QUADS, 5 * (q + 1)))
                        if m_user is not None:
                            pe.wait_ge(*m_user)
                        for qb in range(NT):
                            last = pe.transpose(m_bf[0:12, qb * P:(qb + 1) * P],
                                                mpart[:, qb, :, :].rearrange("p s h -> p (s h)"), ident_b[:, :])
                        last.then_inc(s_mT, 1)
                        m_user = (s_mrow, at(b, QUADS, q + 1))
                    elif kind == "OT":
                        q = step[1]
                        pe.wait_ge(s_o, at(b, QUADS, q + 1))
                        if m_user is not None:
                            pe.wait_ge(*m_user)
                        for t in range(NT):
                            last = pe.transpose(M_BANK[:, t * P:(t + 1) * P], o_t[:, t * P:(t + 1) * P], ident[:, :])
                        last.then_inc(s_oT, 1)
                        m_user = (s_att, at(b, QUADS, q + 1))
                    elif kind == "XT":
                        xt(nxt, slot)
                        user[r] = (s_xtlo, at(nxt, 1, 1))
                pe.wait_ge(s_att, at(b, QUADS, QUADS))
                pe.wait_ge(*user[0])
                transpose_rows(ring[0], att).then_inc(s_aT, 1)
                pe.wait_ge(s_athi, at(b, 1, 1))
                pe.wait_ge(s_atlo, at(b, 1, 1))
                for t in range(NT):
                    dst = ring[0][:, t // 2, (t % 2) * D:(t % 2 + 1) * D]
                    tok = slice(t * P, (t + 1) * P)
                    for k in range(KD):
                        last = split_product(dst, ht_hi[:, k, tok], ht_lo[:, k, tok],
                                             weight(w_hi, C_O, k, D, 0, D), weight(w_lo, C_O, k, D, 0, D),
                                             k == 0, k == KD - 1)
                last.then_inc(s_op, 1)

            def ffn(b, nxt):
                pe.wait_ge(s_xn2, at(b, NT, NT))
                if nxt is not None:
                    pe.wait_ge(s_vsb, at(nxt, NT, NT))
                transpose_rows(ring[0], xn2).then_inc(s_hT, 1)
                pe.wait_ge(s_hthi, at(b, 1, 1))
                pe.wait_ge(s_htlo, at(b, 1, 1))
                for t in range(NT):
                    tok = slice(t * P, (t + 1) * P)
                    dst = M_BANK[:, t * E:(t + 1) * E]
                    for k in range(KD):
                        g_hi, g_lo = weight(w_hi, C_GATE, k, E, 0, E), weight(w_lo, C_GATE, k, E, 0, E)
                        pe.matmul(dst, ht_lo[:, k, tok], g_lo, start=(k == 0), stop=False)
                        last = split_product(dst, ht_hi[:, k, tok], ht_lo[:, k, tok], g_hi, g_lo, False, k == KD - 1)
                last.then_inc(s_logit, 1)

                def gate_up(u):
                    if u < 2 and nxt is not None:
                        pe.wait_ge(s_rot, at(nxt, 8, 4 * u + 4))
                    if u == 2:
                        pe.wait_ge(s_score, at(b, 1, 1))
                    if u >= 3:
                        pe.wait_ge(s_t, at(b, UNITS, u - 2))
                    if u >= SHARED:
                        pe.wait_ge(s_wls, at(b, E, u - SHARED + 1))
                    for n in range(2):
                        for k in range(KD):
                            if u < SHARED:
                                c = (C_SG, C_SU)[n]
                                hi, lo = weight(w_hi, c, k, D, u * P, P), weight(w_lo, c, k, D, u * P, P)
                            else:
                                c = (n * KD + k) * FI
                                hi, lo = gu_hi[:, u % 2, c:c + FI], gu_lo[:, u % 2, c:c + FI]
                            last = split_product(ring[1 + u % 3][:, n, :], hi, lo, ht_hi[:, k, :], ht_lo[:, k, :],
                                                 k == 0, k == KD - 1)
                    last.then_inc(s_gu, 1)

                def down(u):
                    if u == 0:
                        pe.wait_ge(s_cwrow, at(b, 1, 1))
                    pe.wait_ge(s_alo, at(b, UNITS, u + 1))
                    if u < SHARED:
                        hi, lo = weight(w_hi, C_SD, u, D, 0, D), weight(w_lo, C_SD, u, D, 0, D)
                    else:
                        hi, lo = dn_hi[:, u % 3, :], dn_lo[:, u % 3, :]
                    for t in range(NT):
                        tok = slice(t * P, (t + 1) * P)
                        last = split_product(ring[0][:, t // 2, (t % 2) * D:(t % 2 + 1) * D],
                                             a_hi[:, u % 2, tok], a_lo[:, u % 2, tok], hi, lo,
                                             u == 0 and t % 2 == 0, u == UNITS - 1, skip_group_check=True)
                    last.then_inc(s_d, 1)

                gate_up(0)
                gate_up(1)
                pe.wait_ge(s_cw, at(b, 1, 1))
                for t in range(NT):
                    last = pe.transpose(ring[0][0:E, 0, t * P:(t + 1) * P], cw[:, t, :], ident[:, :])
                last.then_inc(s_cwT, 1)
                for u in range(UNITS):
                    if u + 2 < UNITS:
                        gate_up(u + 2)
                    down(u)

            xt(0, ring[0])
            project(0, first=True)
            with pe.Fori(0, B - 1) as i:
                attend(i, i + 1)
                project(i + 1)
                ffn(i, i + 1)
            attend(B - 1, None)
            ffn(B - 1, None)


N_STAT = 2 * NT + 1
LN_STEPS = 6 * NT
ROUTE_STEPS = 28
FLN = 4 * NT


def pack_small(w_q, w_k, w_v, w_o, gate_w, ws_g, ws_u, ws_d):
    def halves(w):
        pairs = w.reshape(H, HALF, 2, D)
        return [pairs[:, :, 0].reshape(P, D).T, pairs[:, :, 1].reshape(P, D).T]

    def tiles(wt):
        return [wt[k * P:(k + 1) * P] for k in range(KD)]

    qkv = np.concatenate(halves(w_q) + halves(w_k) + [w_v.T], axis=1)
    cols = []
    for wt in (qkv, w_o.T, ws_g.T, ws_u.T, ws_d.T, gate_w.T):
        cols += tiles(wt)
    return np.ascontiguousarray(np.concatenate(cols, axis=1))


def pack_experts(wg, wu, wd):
    cols = []
    for e in range(E):
        for w in (wg[e].T, wu[e].T):
            cols += [w[k * P:(k + 1) * P] for k in range(KD)]
        cols.append(wd[e].T)
    return np.ascontiguousarray(np.concatenate(cols, axis=1))


def rope_tables():
    inv = (np.float32(10000.0) ** (np.float32(-2.0) * np.arange(HALF, dtype=np.float32) / np.float32(DH))).astype(np.float32)
    ang = np.arange(T, dtype=np.float32)[None, :] * np.tile(inv, H)[:, None]
    return np.ascontiguousarray(np.stack([np.cos(ang), np.sin(ang)], axis=1).astype(np.float32))


def tie_tables():
    def lower(n):
        return (np.arange(n)[None, :] < np.arange(n)[:, None]).astype(np.float32).reshape(-1)

    row = np.concatenate([lower(E), lower(NG)])
    return np.ascontiguousarray(np.broadcast_to(row, (P, row.size)))


def kernel(L0_attn_x, L0_attn_W_q, L0_attn_W_k, L0_attn_W_v, L0_attn_W_o, L0_ffn_gate_w, L0_ffn_gate_bias,
           L0_ffn_Wg, L0_ffn_Wu, L0_ffn_Wd, L0_ffn_Ws_g, L0_ffn_Ws_u, L0_ffn_Ws_d):
    import concourse.bacc as bacc
    from concourse.bass_utils import run_bass_kernel_spmd

    a = np.asarray
    arrays = {
        "x": np.ascontiguousarray(a(L0_attn_x)),
        "w_small": pack_small(a(L0_attn_W_q), a(L0_attn_W_k), a(L0_attn_W_v), a(L0_attn_W_o), a(L0_ffn_gate_w),
                              a(L0_ffn_Ws_g), a(L0_ffn_Ws_u), a(L0_ffn_Ws_d)),
        "w_exp": pack_experts(a(L0_ffn_Wg), a(L0_ffn_Wu), a(L0_ffn_Wd)),
        "rope": rope_tables(),
        "ties": tie_tables(),
        "bias": np.ascontiguousarray(np.broadcast_to(a(L0_ffn_gate_bias), (P, NT, E)).reshape(P, NT * E)),
    }
    nc = bacc.Bacc("TRN2", target_bir_lowering=False, num_devices=1)
    ins = [nc.dram_tensor(n, v.shape, mybir.dt.from_np(v.dtype), kind="ExternalInput").ap() for n, v in arrays.items()]
    out = nc.dram_tensor("out", (B, T, D), mybir.dt.float32, kind="ExternalOutput").ap()
    block_kernel(nc, *ins, out)
    r = run_bass_kernel_spmd(nc, [arrays], core_ids=[0])
    return r.results[0]["out"]
```

```python
import numpy as np
import concourse.bass as bass
from concourse import mybir
from contextlib import ExitStack

B, T, D = 8, 512, 256
P = 128
NT = T // P
KD = D // P
H, DH = 16, 16
HALF = DH // 2
QUADS, PAIRS = H // 4, H // 2
E, FI, TOPK, NG = 16, 128, 4, 4
EPG = E // NG
SHARED = 2
UNITS = SHARED + E
EPS = 1e-5
ROUTE_SCALE = 2.5
SCALE = DH ** -0.5
MASKED = -1e38
BIG = 1e30

Q_PART = [0, 0, 0, 1, 1, 2]
K_PART = [0, 1, 2, 0, 1, 0]
SLOTS = len(Q_PART)
ROWS = SLOTS * DH
MROWS = ROWS + 3

C_QKV = 0
C_O = C_QKV + KD * 3 * D
C_SG = C_O + KD * D
C_SU = C_SG + KD * D
C_SD = C_SU + KD * D
C_GATE = C_SD + KD * D
C_ALL = C_GATE + KD * E
GU_COLS = KD * FI * 2
EXP_COLS = GU_COLS + D

ROT = [(0, 1, 2, 3), (4, 5, 1, 3)]
SUM = [0, 2, 4, 1]
SPARE = [3, 5]
PART_UNIT = 2

N_S = PAIRS * NT
N_ST = QUADS * NT * 2
N_AV = QUADS * NT
N_STACK = 2 * 2 * SLOTS


def attention_plan():
    plan = [("S", 0, qb) for qb in range(NT)] + [("S", 1, qb) for qb in range(NT)]
    plan += [("S", 2, qb) for qb in range(NT)][:2] + [("MT", 0)] + [("S", 2, qb) for qb in range(NT)][2:]
    s_rest = [("S", p, qb) for p in range(3, PAIRS) for qb in range(NT)]
    for q in range(QUADS):
        for kb in range(NT):
            for half in range(2):
                plan.append(("ST", q, kb, half))
                if s_rest:
                    plan.append(s_rest.pop(0))
            if kb >= 1:
                plan.append(("AV", q, kb - 1))
            elif q >= 1:
                plan += [("AV", q - 1, NT - 1)]
            if kb == 1 and q >= 1:
                plan.append(("OT", q - 1))
            if kb == 2 and q + 1 < QUADS:
                plan.append(("MT", q + 1))
        if q == 1:
            plan.append(("XT",))
        if q == 0:
            plan.append(("LN",))
    plan += [("AV", QUADS - 1, NT - 1), ("OT", QUADS - 1)]
    return plan


PLAN = attention_plan()


def block_kernel(nc, x, w_small, w_exp, rope, ties, bias, out):
    fp32, fp32r, bf16 = mybir.dt.float32, mybir.dt.float32r, mybir.dt.bfloat16
    ALU, ACT, AX = mybir.AluOpType, mybir.ActivationFunctionType, mybir.AxisListType

    ctx = ExitStack()
    with ctx:
        def sb(name, shape, dt=fp32):
            return ctx.enter_context(nc.sbuf_tensor(name, shape, dt))

        def sem(name):
            return ctx.enter_context(nc.semaphore(name))

        part_dram = nc.dram_tensor("part_scratch", (4, P, 3, T), bf16, kind="Internal").ap()
        cw_dram = nc.dram_tensor("cw_scratch", (E, T), fp32, kind="Internal").ap()

        w_hi = sb("w_hi", [P, C_ALL], fp32r)
        w_lo = sb("w_lo", [P, C_ALL], fp32r)
        w_raw = sb("w_raw", [P, E * EXP_COLS])
        gu_hi = sb("gu_hi", [P, 2, 2 * KD * FI], fp32r)
        gu_lo = sb("gu_lo", [P, 2, 2 * KD * FI], fp32r)
        dn_hi = sb("dn_hi", [P, 2, D], fp32r)
        dn_lo = sb("dn_lo", [P, 2, D], fp32r)
        rope_t = sb("rope_t", [P, 2, T])
        tie_t = sb("tie_t", [P, E * E + NG * NG])
        bias_t = sb("bias_t", [P, NT * E])
        ident = sb("ident", [P, P])
        ident_b = sb("ident_b", [P, P], bf16)
        mask_b = sb("mask_b", [P, P], bf16)
        minus_half = sb("minus_half", [P, NT])
        x_ln = sb("x_ln", [P, NT, D])
        xn = x_ln
        st1 = sb("st1", [P, NT, 6])
        mv1 = sb("mv1", [P, NT, 2])
        ve1 = sb("ve1", [P, NT])
        rstd1 = sb("rstd1", [P, NT])
        xt_hi = sb("xt_hi", [P, KD, T], fp32r)
        xt_lo = sb("xt_lo", [P, KD, T], fp32r)
        rot = sb("rot", [P, 6, T])
        part = sb("part", [P, 2, 2, 3, T], bf16)
        q_st = sb("q_st", [P, H, T], bf16)
        k_st = sb("k_st", [P, H, T], bf16)
        v_sb = sb("v_sb", [P, NT, H, 32])
        nmax = sb("nmax", [P, NT, H])
        mres = sb("mres", [P, 2, NT, 4])
        mpart = sb("mpart", [P, NT, 3, 4], bf16)
        mrow = rot[:, 5, :].bitcast(bf16)[0:12, 0:T]
        prob = sb("prob", [P, 2, 4, T])
        mask_f = prob[:, 0, 0, 0:P]
        o_t = sb("o_t", [P, T])
        rden = sb("rden", [P, NT, 4])
        ht_hi = sb("ht_hi", [P, KD, T], fp32r)
        ht_lo = sb("ht_lo", [P, KD, T], fp32r)
        x1 = sb("x1", [P, NT, D])
        xn2 = sb("xn2", [P, NT, D])
        att = xn2
        st2 = sb("st2", [P, NT, 6])
        mv2 = sb("mv2", [P, NT, 2])
        ve2 = sb("ve2", [P, NT])
        rstd2 = sb("rstd2", [P, NT])
        r_sc = sb("r_sc", [P, NT * E])
        r_sf = sb("r_sf", [P, NT * E])
        r_hi = sb("r_hi", [P, NT * NG, 2])
        r_lo = sb("r_lo", [P, NT * NG, 2])
        r_g = sb("r_g", [P, 5, NT * NG])
        r_b = prob[:, 0, 0:2, :].rearrange("p a n -> p (a n)")
        r_c = prob[:, 0, 2:4, :].rearrange("p a n -> p (a n)")
        r_d = sb("r_d", [P, 2, NT * E])
        cw = sb("cw", [P, NT, E])
        r_s = sb("r_s", [P, 3, NT])
        cw_t = o_t[0:E, :]
        cwb, silu, act = prob[:, 0, :, :], prob[:, 1, 0:2, :], prob[:, 1, 2:4, :]
        a_hi, a_lo = xt_hi, xt_lo
        stage = q_st[:, :, :].rearrange("p h n -> p (h n)").bitcast(fp32)[:, 0:C_ALL]

        ring = [ctx.enter_context(nc.psum_tensor(f"ring{i}", [P, 2, T], fp32)) for i in range(4)]
        O_BANK, M_BANK = ring[3][:, 0, :], ring[3][:, 1, :]
        m_bf = M_BANK.bitcast(bf16)

        s_small = sem("small_loaded")
        s_const = sem("constants_loaded")
        s_wexp = sem("experts_loaded")
        s_pool0 = sem("pool_constants")
        s_dve0 = sem("dve_constants")
        s_whi = sem("weights_high")
        s_wlo = sem("weights_low")
        s_seen_dve = sem("waited_dve")
        s_seen_pool = sem("waited_pool")
        s_x = sem("x_loaded")
        s_stat1 = sem("stats1")
        s_pow1 = sem("rstd1_ready")
        s_xn = sem("xn_ready")
        s_xnT = sem("xn_transposed")
        s_xthi = sem("xt_high")
        s_xtlo = sem("xt_low")
        s_qk = sem("qk_products")
        s_v = sem("v_products")
        s_vsb = sem("v_copied")
        s_rot = sem("rotary_products")
        s_sum = sem("rotary_sums")
        s_phi = sem("part_high")
        s_pres = sem("part_residual")
        s_pmid = sem("part_middle")
        s_plo = sem("part_low")
        s_pout = [sem(f"parts_stored{n}") for n in range(4)]
        s_stack = sem("stacked")
        s_S = sem("scores")
        s_max = sem("row_maxima")
        s_mp = sem("maxima_split")
        s_mT = sem("maxima_transposed")
        s_mrow = sem("maxima_rows")
        s_mdma = sem("maxima_stacked")
        s_ST = sem("scores_transposed")
        s_exp = sem("exponentials")
        s_tri = sem("diagonal_cut")
        s_av = sem("pv_step")
        s_o = sem("o_copied")
        s_oT = sem("o_transposed")
        s_rden = sem("denominators")
        s_att = sem("attention_rows")
        s_aT = sem("attention_transposed")
        s_athi = sem("at_high")
        s_atlo = sem("at_low")
        s_op = sem("o_projected")
        s_x1in = sem("x1_loaded")
        s_ln = sem("ln_steps")
        s_lnv = sem("ln_variance")
        s_lnr = sem("ln_rstd")
        s_xn2 = sem("xn2_ready")
        s_hT = sem("xn2_transposed")
        s_hthi = sem("ht_high")
        s_htlo = sem("ht_low")
        s_logit = sem("logits")
        s_score = sem("router_scores")
        s_route = sem("router_steps")
        s_cw = sem("gates_ready")
        s_cwT = sem("gates_transposed")
        s_cwrow = sem("gates_rows")
        s_cwout = sem("gates_stored")
        s_cwb = [sem(f"gates_broadcast{i}") for i in range(4)]
        s_guhi = sem("gate_up_weights_high")
        s_gulo = sem("gate_up_weights_low")
        s_dnhi = sem("down_weights_high")
        s_dnlo = sem("down_weights_low")
        s_gu = sem("gate_up")
        s_silu = sem("silu")
        s_t = sem("silu_times_up")
        s_a = sem("gated")
        s_ahi = sem("act_high")
        s_alo = sem("act_low")
        s_d = sem("down")
        s_y = sem("y_read")
        s_fln = sem("final_ln_steps")
        s_fv = sem("final_variance")
        s_fr = sem("final_rstd")
        s_out = sem("out_stored")

        def at(b, per_seq, n):
            return b * per_seq + n

        def seq(b):
            return bass.ds(b, 1) if not isinstance(b, int) else slice(b, b + 1)

        def expert(u, col, n):
            c = (u - SHARED) * EXP_COLS + col
            return w_raw[:, c:c + n]

        block = ctx.enter_context(nc.Block())

        @block.sync
        def _(sp):
            sp.dma_start(stage, w_small).then_inc(s_small, 16)

            def load_x(b, first=False):
                if not first:
                    sp.wait_ge(s_xnT, b)
                sp.dma_start(x_ln[:, :, :], x[seq(b)].rearrange("a (t p) d -> p (a t) d", p=P)).then_inc(s_x, 16)

            def load_x1(b):
                sp.dma_start(x1[:, :, :], x[seq(b)].rearrange("a (t p) d -> p (a t) d", p=P)).then_inc(s_x1in, 16)

            def store_parts(b, n):
                sp.wait_ge(s_plo, at(b, 4, n + 1))
                sp.dma_start(part_dram[n], part[:, n // 2, n % 2, :, :]).then_inc(s_pout[n], 16)

            def stack(b, n):
                dst, parts = ((q_st, Q_PART), (k_st, K_PART))[n // 2]
                sp.wait_ge(s_pout[n], at(b, 16, 16))
                for s in range(SLOTS):
                    r = s * DH + (n % 2) * HALF
                    by_pair = part_dram[n, :, parts[s], :].rearrange("(h j) t -> j h t", j=HALF)
                    sp.dma_start(dst[r:r + HALF, :, :], by_pair).then_inc(s_stack, 16)

            def attend(b):
                for q in range(QUADS):
                    sp.wait_ge(s_mrow, at(b, QUADS, q + 1))
                    sp.dma_start(q_st[ROWS:MROWS, 4 * q:4 * q + 4, :],
                                 mrow[:, :]).then_inc(s_mdma, 16)

            def ffn(b, nxt):
                sp.wait_ge(s_cwrow, at(b, 1, 1))
                sp.dma_start(cw_dram, cw_t[:, :]).then_inc(s_cwout, 16)
                sp.wait_ge(s_cwout, at(b, 16, 16))
                for e in range(E):
                    if nxt is not None and 6 <= e < 10:
                        store_parts(nxt, e - 6)
                    if nxt is not None and 8 <= e < 12:
                        if e == 8:
                            sp.wait_ge(s_ST, nxt * N_ST)
                        stack(nxt, e - 8)
                    if e >= 4:
                        sp.wait_ge(s_a, at(b, E, e - 3))
                    sp.dma_start(cwb[:, e % 4, :], cw_dram[e:e + 1, :].to_broadcast([P, T])).then_inc(s_cwb[e % 4], 16)
                sp.wait_ge(s_fln, at(b, FLN, FLN))
                sp.dma_start(out[seq(b)].rearrange("a (t p) d -> p (a t) d", p=P), xn2[:, :, :]).then_inc(s_out, 16)
                sp.wait_ge(s_out, at(b, 16, 16))

            load_x(0, first=True)
            sp.dma_start(rope_t[:, :, :], rope).then_inc(s_const, 16)
            sp.dma_start(tie_t[:, :], ties).then_inc(s_const, 16)
            sp.dma_start(bias_t[:, :], bias).then_inc(s_const, 16)
            load_x1(0)
            for e in range(0, E, 4):
                sp.dma_start(w_raw[:, e * EXP_COLS:(e + 4) * EXP_COLS], w_exp[:, e * EXP_COLS:(e + 4) * EXP_COLS]
                             ).then_inc(s_wexp, 16)
            sp.wait_ge(s_wlo, 1)
            for n in range(4):
                store_parts(0, n)
            for n in range(4):
                stack(0, n)
            with sp.Fori(0, B - 1) as i:
                load_x(i + 1)
                attend(i)
                ffn(i, i + 1)
                load_x1(i + 1)
            attend(B - 1)
            ffn(B - 1, None)

        @block.gpsimd
        def _(pool):
            pool.memset(ident[:, :], 0.0).then_inc(s_pool0, 1)
            pool.memset(mask_f, 0.0).then_inc(s_pool0, 1)
            pool.memset(minus_half[:, :], -0.5).then_inc(s_pool0, 1)
            pool.memset(v_sb[:, :, :, :], 0.0).then_inc(s_pool0, 1)
            pool.memset(k_st[:, :, :], 1.0).then_inc(s_pool0, 1)
            pool.wait_ge(s_pool0, 5)
            pool.affine_select(out=ident[:, :], in_=ident[:, :], compare_op=ALU.not_equal, fill=1.0,
                               base=0, pattern=[[-1, P]], channel_multiplier=1).then_inc(s_pool0, 1)
            pool.affine_select(out=mask_f, in_=mask_f, compare_op=ALU.is_ge, fill=MASKED,
                               base=0, pattern=[[-1, P]], channel_multiplier=1).then_inc(s_pool0, 1)
            pool.memset(v_sb[:, :, :, DH:DH + 1], 1.0).then_inc(s_pool0, 1)

            def norm(b):
                pool.wait_ge(s_stat1, at(b, N_STAT, N_STAT))
                pool.tensor_tensor(rstd1[:, :], ve1[:, :], minus_half[:, :], ALU.pow).then_inc(s_pow1, 1)

            def project(b):
                for qk in range(2):
                    ec, os, es, oc = ROT[qk]
                    pool.wait_ge(s_rot, at(b, 8, 4 * qk + 2))
                    pool.tensor_tensor(rot[:, ec, :], rot[:, ec, :], rot[:, os, :], ALU.subtract).then_inc(s_sum, 1)
                    pool.wait_ge(s_rot, at(b, 8, 4 * qk + 4))
                    pool.tensor_tensor(rot[:, es, :], rot[:, es, :], rot[:, oc, :], ALU.add).then_inc(s_sum, 1)

            def attend(b, nxt):
                for u in range(N_AV):
                    if u == NT and nxt is not None:
                        norm(nxt)
                    pool.wait_ge(s_exp, at(b, N_ST, 2 * u + 2))
                    pool.sem_inc(s_seen_pool, 1)
                    diag = prob[:, u % 2, :, 0:P]
                    pool.affine_select(out=diag, in_=diag, compare_op=ALU.is_ge, fill=0.0, base=0,
                                       pattern=[[0, 4], [1, P]], channel_multiplier=-1).then_inc(s_tri, 1)
                for n in range(2):
                    pool.wait_ge(s_lnv, at(b, 2, n + 1))
                    pool.tensor_tensor(rstd2[:, :], ve2[:, :], minus_half[:, :], ALU.pow).then_inc(s_lnr, 1)

            def ffn(b):
                def gate_up_low(u):
                    pool.wait_ge(s_guhi, at(b, E, u - SHARED + 1))
                    pool.tensor_tensor(gu_lo[:, u % 2, :], expert(u, 0, GU_COLS), gu_hi[:, u % 2, :],
                                       ALU.subtract).then_inc(s_gulo, 1)

                def down_low(u):
                    pool.wait_ge(s_dnhi, at(b, E, u - SHARED + 1))
                    pool.tensor_tensor(dn_lo[:, u % 2, :], expert(u, GU_COLS, D), dn_hi[:, u % 2, :],
                                       ALU.subtract).then_inc(s_dnlo, 1)

                for u in range(UNITS + 1):
                    for v in ((SHARED, SHARED + 1) if u == 0 else (u + 2,)):
                        if SHARED <= v < UNITS and not (u == 1 and v == 3):
                            gate_up_low(v)
                    if u - 1 >= SHARED:
                        down_low(u - 1)
                pool.wait_ge(s_fv, at(b, 1, 1))
                pool.tensor_tensor(rstd2[:, :], ve2[:, :], minus_half[:, :], ALU.pow).then_inc(s_fr, 1)

            norm(0)
            project(0)
            with pool.Fori(0, B - 1) as i:
                attend(i, i + 1)
                project(i + 1)
                ffn(i)
            attend(B - 1, None)
            ffn(B - 1)

        @block.vector
        def _(dve):
            dve.wait_ge(s_pool0, 8)
            dve.tensor_copy(ident_b[:, :], ident[:, :]).then_inc(s_dve0, 1)
            dve.tensor_copy(mask_b[:, :], mask_f).then_inc(s_dve0, 1)
            dve.wait_ge(s_whi, 1)
            dve.tensor_tensor(w_lo[:, :], stage, w_hi[:, :], ALU.subtract).then_inc(s_wlo, 1)

            def norm(b):
                dve.wait_ge(s_x, at(b, 16, 16))
                for t in range(NT):
                    dve.bn_stats(st1[:, t, :], x_ln[:, t, :]).then_inc(s_stat1, 1)
                for t in range(NT):
                    dve.wait_ge(s_stat1, at(b, N_STAT, t + 1))
                    dve.sem_inc(s_seen_dve, 1)
                    dve.bn_aggr(mv1[:, t, :], st1[:, t, :]).then_inc(s_stat1, 1)
                dve.wait_ge(s_stat1, at(b, N_STAT, 2 * NT))
                dve.tensor_scalar(ve1[:, :], mv1[:, :, 1], EPS, None, ALU.add).then_inc(s_stat1, 1)
                dve.wait_ge(s_pow1, at(b, 1, 1))
                for t in range(NT):
                    dve.tensor_scalar(xn[:, t, :], x_ln[:, t, :], mv1[:, t, 0:1], rstd1[:, t:t + 1],
                                      ALU.subtract, ALU.mult).then_inc(s_xn, 1)

            def xt_low(b, slot):
                dve.wait_ge(s_xthi, at(b, 1, 1))
                dve.tensor_tensor(xt_lo[:, :, :], slot[:, :, :], xt_hi[:, :, :], ALU.subtract).then_inc(s_xtlo, 1)

            def project(b, first=False):
                if first:
                    dve.wait_ge(s_const, 48)
                cos, sin = rope_t[:, 0, :], rope_t[:, 1, :]
                for qk in range(2):
                    dve.wait_ge(s_qk, at(b, 2, qk + 1))
                    even, odd = ring[1 + qk][:, 0, :], ring[1 + qk][:, 1, :]
                    for n, (src, tab) in enumerate(((even, cos), (odd, sin), (even, sin), (odd, cos))):
                        if qk and n >= 2:
                            dve.wait_ge(s_sum, at(b, 4, n - 1))
                        dve.tensor_tensor(rot[:, ROT[qk][n], :], src, tab, ALU.mult).then_inc(s_rot, 1)

            def part_residual(b, n):
                dve.wait_ge(s_phi, at(b, 4, n + 1))
                if n == 0:
                    dve.wait_ge(s_sum, at(b, 4, 4))
                if n >= 2:
                    dve.wait_ge(s_plo, at(b, 4, n - 1))
                dve.tensor_tensor(rot[:, SPARE[n % 2], :], rot[:, SUM[n], :], part[:, n // 2, n % 2, 0, :],
                                  ALU.subtract).then_inc(s_pres, 1)

            def part_low(b, n):
                dve.wait_ge(s_pmid, at(b, 4, n + 1))
                dve.tensor_tensor(part[:, n // 2, n % 2, 2, :], rot[:, SPARE[n % 2], :], part[:, n // 2, n % 2, 1, :],
                                  ALU.subtract).then_inc(s_plo, 1)

            def parts_step(b, n):
                if n < 4:
                    part_residual(b, n)
                if n >= 1:
                    part_low(b, n - 1)

            def row_max(b, n_s, slot, pair, qb):
                dve.wait_ge(s_S, at(b, N_S, n_s + 1))
                n = (qb + 1) * P
                dve.tensor_reduce(nmax[:, qb, 2 * pair:2 * pair + 2], slot[:, :, 0:n], AX.X, ALU.max,
                                  negate=True).then_inc(s_max, 1)

            def split_max(b, q):
                full = nmax[:, :, 4 * q:4 * q + 4]
                dve.wait_ge(s_max, at(b, N_S, (2 * q + 2) * NT))
                if q:
                    dve.wait_ge(s_mT, at(b, QUADS, q))
                base = 5 * q
                dve.tensor_copy(mpart[:, :, 0, :], full).then_inc(s_mp, 1)
                dve.wait_ge(s_mp, at(b, 5 * QUADS, base + 1))
                dve.tensor_tensor(mres[:, 0, :, :], full, mpart[:, :, 0, :], ALU.subtract).then_inc(s_mp, 1)
                dve.wait_ge(s_mp, at(b, 5 * QUADS, base + 2))
                dve.tensor_copy(mpart[:, :, 1, :], mres[:, 0, :, :]).then_inc(s_mp, 1)
                dve.wait_ge(s_mp, at(b, 5 * QUADS, base + 3))
                dve.tensor_tensor(mres[:, 1, :, :], mres[:, 0, :, :], mpart[:, :, 1, :],
                                  ALU.subtract).then_inc(s_mp, 1)
                dve.wait_ge(s_mp, at(b, 5 * QUADS, base + 4))
                dve.tensor_copy(mpart[:, :, 2, :], mres[:, 1, :, :]).then_inc(s_mp, 1)

            def head_rows(b, q):
                o = M_BANK.rearrange("p (t h c) -> p t h c", t=NT, h=4)
                dve.wait_ge(s_oT, at(b, QUADS, q + 1))
                if q == 0:
                    dve.wait_ge(s_x1in, at(b, 16, 16))
                dve.reciprocal(rden[:, :, :], o[:, :, :, DH]).then_inc(s_rden, 1)
                dve.wait_ge(s_rden, at(b, QUADS, q + 1))
                dst = att[:, :, :].rearrange("p t (h c) -> p t h c", c=DH)[:, :, 4 * q:4 * q + 4, :]
                dve.tensor_tensor(dst, o[:, :, :, 0:DH], rden[:, :, :].unsqueeze(3).to_broadcast([P, NT, 4, DH]),
                                  ALU.mult).then_inc(s_att, 1)

            def statistics(src, step, value, v_sem, total, b):
                for t in range(NT):
                    dve.bn_stats(st2[:, t, :], src(t)).then_inc(step, 1)
                for t in range(NT):
                    dve.wait_ge(step, at(b, total, value + t + 1))
                    dve.sem_inc(s_seen_dve, 1)
                    dve.bn_aggr(mv2[:, t, :], st2[:, t, :]).then_inc(step, 1)
                dve.wait_ge(step, at(b, total, value + 2 * NT))
                dve.tensor_scalar(ve2[:, :], mv2[:, :, 1], EPS, None, ALU.add).then_inc(v_sem, 1)

            def attend(b, nxt):
                n_s = n = 0
                for step in PLAN:
                    if step[0] in ("S", "ST", "XT"):
                        slot = ring[(n + 1) % 3]
                        n += 1
                    if step[0] == "S":
                        row_max(b, n_s, slot, step[1], step[2])
                        n_s += 1
                    elif step[0] == "MT":
                        split_max(b, step[1])
                    elif step[0] == "OT":
                        head_rows(b, step[1])
                    elif step[0] == "LN" and nxt is not None:
                        norm(nxt)
                    elif step[0] == "XT" and nxt is not None:
                        xt_low(nxt, slot)
                dve.wait_ge(s_athi, at(b, 1, 1))
                dve.tensor_tensor(ht_lo[:, :, :], ring[0][:, :, :], ht_hi[:, :, :], ALU.subtract).then_inc(s_atlo, 1)
                proj = ring[0][:, :, :].rearrange("p a (c d) -> p (a c) d", d=D)
                dve.wait_ge(s_op, at(b, 1, 1))
                statistics(lambda t: proj[:, t, :], s_ln, 0, s_lnv, LN_STEPS, b)
                dve.wait_ge(s_lnr, at(b, 2, 1))
                for t in range(NT):
                    dve.tensor_scalar(xn2[:, t, :], proj[:, t, :], mv2[:, t, 0:1], rstd2[:, t:t + 1],
                                      ALU.subtract, ALU.mult).then_inc(s_ln, 1)
                for t in range(NT):
                    dve.wait_ge(s_ln, at(b, LN_STEPS, 2 * NT + t + 1))
                    dve.tensor_tensor(x1[:, t, :], x1[:, t, :], xn2[:, t, :], ALU.add).then_inc(s_ln, 1)
                dve.wait_ge(s_ln, at(b, LN_STEPS, 4 * NT))
                statistics(lambda t: x1[:, t, :], s_ln, 4 * NT, s_lnv, LN_STEPS, b)
                dve.wait_ge(s_lnr, at(b, 2, 2))
                for t in range(NT):
                    dve.tensor_scalar(xn2[:, t, :], x1[:, t, :], mv2[:, t, 0:1], rstd2[:, t:t + 1],
                                      ALU.subtract, ALU.mult).then_inc(s_xn2, 1)

            def route(b):
                count = [0]

                def step(ins):
                    count[0] += 1
                    ins.then_inc(s_route, 1)
                    dve.wait_ge(s_route, at(b, ROUTE_STEPS, count[0]))

                def beaten(rank, v, n, tie, wide_a, wide_b):
                    other = v.unsqueeze(2).to_broadcast([P, NT, n, n])
                    own = v.unsqueeze(3).to_broadcast([P, NT, n, n])
                    a = wide_a[:, 0:NT * n * n].rearrange("p (t g k) -> p t g k", t=NT, g=n)
                    c = wide_b[:, 0:NT * n * n].rearrange("p (t g k) -> p t g k", t=NT, g=n)
                    tb = tie.rearrange("p (g k) -> p g k", g=n).unsqueeze(1).to_broadcast([P, NT, n, n])
                    step(dve.tensor_tensor(a, other, own, ALU.is_equal))
                    step(dve.tensor_tensor(a, a, tb, ALU.mult))
                    step(dve.tensor_tensor(c, other, own, ALU.is_gt))
                    step(dve.tensor_tensor(a, a, c, ALU.add))
                    step(dve.tensor_reduce(rank, a, AX.X, ALU.add))

                t_e = lambda ap: ap.rearrange("p (t e) -> p t e", t=NT)
                t_g = lambda ap: ap.rearrange("p (t g) -> p t g", t=NT)
                grouped = lambda ap: ap.rearrange("p (g k) -> p g k", k=EPG)
                dve.wait_ge(s_score, at(b, 1, 1))
                step(dve.tensor_tensor(r_sf[:, :], r_sc[:, :], bias_t[:, :], ALU.add))
                quad = grouped(r_sf[:, :]).rearrange("p g (a c) -> p g a c", a=2)
                step(dve.tensor_tensor(r_hi[:, :, :], quad[:, :, :, 0], quad[:, :, :, 1], ALU.max))
                step(dve.tensor_tensor(r_lo[:, :, :], quad[:, :, :, 0], quad[:, :, :, 1], ALU.min))
                step(dve.tensor_tensor(r_g[:, 0, :], r_hi[:, :, 0], r_hi[:, :, 1], ALU.max))
                step(dve.tensor_tensor(r_g[:, 1, :], r_hi[:, :, 0], r_hi[:, :, 1], ALU.min))
                step(dve.tensor_tensor(r_g[:, 2, :], r_lo[:, :, 0], r_lo[:, :, 1], ALU.max))
                step(dve.tensor_tensor(r_g[:, 1, :], r_g[:, 1, :], r_g[:, 2, :], ALU.max))
                step(dve.tensor_tensor(r_g[:, 0, :], r_g[:, 0, :], r_g[:, 1, :], ALU.add))
                beaten(t_g(r_g[:, 3, :]), t_g(r_g[:, 0, :]), NG, tie_t[:, E * E:], r_b, r_c)
                step(dve.tensor_scalar(r_g[:, 3, :], r_g[:, 3, :], 1.5, None, ALU.is_lt))
                step(dve.tensor_scalar(r_g[:, 4, :], r_g[:, 3, :], BIG, -BIG, ALU.mult, ALU.add))
                wide = [P, NT * NG, EPG]
                step(dve.tensor_tensor(grouped(r_sf[:, :]), grouped(r_sf[:, :]),
                                       r_g[:, 3, :].unsqueeze(2).to_broadcast(wide), ALU.mult))
                step(dve.tensor_tensor(grouped(r_sf[:, :]), grouped(r_sf[:, :]),
                                       r_g[:, 4, :].unsqueeze(2).to_broadcast(wide), ALU.add))
                beaten(t_e(r_d[:, 0, :]), t_e(r_sf[:, :]), E, tie_t[:, 0:E * E], r_b, r_c)
                step(dve.tensor_scalar(r_d[:, 0, :], r_d[:, 0, :], TOPK - 0.5, None, ALU.is_lt))
                step(dve.tensor_tensor(r_d[:, 1, :], r_d[:, 0, :], r_sc[:, :], ALU.mult))
                step(dve.tensor_reduce(r_s[:, 0, :], t_e(r_d[:, 1, :]), AX.X, ALU.add))
                step(dve.tensor_scalar(r_s[:, 1, :], r_s[:, 0, :], 1e-20, None, ALU.add))
                step(dve.reciprocal(r_s[:, 2, :], r_s[:, 1, :]))
                step(dve.tensor_tensor(t_e(r_d[:, 1, :]), t_e(r_d[:, 1, :]),
                                       r_s[:, 2, :].unsqueeze(2).to_broadcast([P, NT, E]), ALU.mult))
                assert count[0] == ROUTE_STEPS
                dve.tensor_scalar(cw[:, :, :], t_e(r_d[:, 1, :]), ROUTE_SCALE, None, ALU.mult).then_inc(s_cw, 1)

            def ffn(b, nxt):
                dve.wait_ge(s_hthi, at(b, 1, 1))
                dve.tensor_tensor(ht_lo[:, :, :], ring[0][:, :, :], ht_hi[:, :, :], ALU.subtract).then_inc(s_htlo, 1)
                route(b)

                def low(u):
                    dve.wait_ge(s_ahi, at(b, UNITS, u + 1))
                    dve.tensor_tensor(a_lo[:, u % 2, :], act[:, u % 2, :], a_hi[:, u % 2, :],
                                      ALU.subtract).then_inc(s_alo, 1)

                for u in range(UNITS):
                    if u >= 2:
                        dve.wait_ge(s_alo, at(b, UNITS, u - 1))
                    dve.wait_ge(s_silu, at(b, UNITS, u + 1))
                    dve.tensor_tensor(act[:, u % 2, :], silu[:, u % 2, :], ring[1 + u % 3][:, 1, :],
                                      ALU.mult).then_inc(s_t, 1)
                    if u >= SHARED:
                        e = u - SHARED
                        dve.wait_ge(s_t, at(b, UNITS, u + 1))
                        dve.wait_ge(s_cwb[e % 4], at(b, 16 * (E // 4), 16 * (e // 4 + 1)))
                        dve.tensor_tensor(act[:, u % 2, :], act[:, u % 2, :], cwb[:, e % 4, :],
                                          ALU.mult).then_inc(s_a, 1)
                    if u >= 1:
                        low(u - 1)
                    if nxt is not None and PART_UNIT <= u < PART_UNIT + 5:
                        parts_step(nxt, u - PART_UNIT)
                low(UNITS - 1)
                y = ring[0][:, :, :].rearrange("p a (c d) -> p (a c) d", d=D)
                dve.wait_ge(s_d, at(b, UNITS, UNITS))
                dve.tensor_tensor(xn2[:, :, :], y, xn2[:, :, :], ALU.add).then_inc(s_y, 1)
                dve.wait_ge(s_y, at(b, 1, 2))
                statistics(lambda t: xn2[:, t, :], s_fln, 0, s_fv, FLN, b)
                dve.wait_ge(s_fr, at(b, 1, 1))
                for t in range(NT):
                    dve.tensor_scalar(xn2[:, t, :], xn2[:, t, :], mv2[:, t, 0:1], rstd2[:, t:t + 1],
                                      ALU.subtract, ALU.mult).then_inc(s_fln, 1)
                for t in range(NT):
                    dve.wait_ge(s_fln, at(b, FLN, 2 * NT + t + 1))
                    dve.tensor_tensor(xn2[:, t, :], xn2[:, t, :], x1[:, t, :], ALU.add).then_inc(s_fln, 1)

            norm(0)
            xt_low(0, ring[0])
            dve.memset(r_s[:, :, :], 0.0).then_inc(s_y, 1)
            project(0, first=True)
            for n in range(5):
                parts_step(0, n)
            with dve.Fori(0, B - 1) as i:
                attend(i, i + 1)
                project(i + 1)
                ffn(i, i + 1)
            attend(B - 1, None)
            ffn(B - 1, None)

        @block.scalar
        def _(act_e):
            act_e.wait_ge(s_small, 16)
            act_e.activation(w_hi[:, :], stage, ACT.Copy).then_inc(s_whi, 1)

            def xt_high(b, slot, first=False):
                act_e.wait_ge(s_xnT, at(b, 1, 1))
                if not first:
                    act_e.wait_ge(s_v, b)
                act_e.activation(xt_hi[:, :, :], slot[:, :, :], ACT.Copy).then_inc(s_xthi, 1)

            def project(b, first=False):
                if first:
                    act_e.wait_ge(s_pool0, 8)
                else:
                    act_e.wait_ge(s_av, b * N_AV)
                act_e.wait_ge(s_v, at(b, 1, 1))
                v = ring[0][:, :, :].rearrange("p a (c h d) -> p (a c) h d", c=2, h=H)
                for t in range(NT):
                    act_e.activation(v_sb[:, t, :, 0:DH], v[:, t, :, :], ACT.Copy).then_inc(s_vsb, 1)

            def parts_step(b, n, first=False):
                if n == 0 and not first:
                    act_e.wait_ge(s_stack, b * N_STACK * 16)
                if n < 4:
                    act_e.wait_ge(s_sum, at(b, 4, n + 1))
                    act_e.activation(part[:, n // 2, n % 2, 0, :], rot[:, SUM[n], :], ACT.Copy).then_inc(s_phi, 1)
                if n >= 1:
                    m = n - 1
                    act_e.wait_ge(s_pres, at(b, 4, m + 1))
                    act_e.activation(part[:, m // 2, m % 2, 1, :], rot[:, SPARE[m % 2], :], ACT.Copy).then_inc(s_pmid, 1)

            def attend(b, nxt):
                n = n_st = 0
                for step in PLAN:
                    if step[0] in ("S", "ST", "XT"):
                        slot = ring[(n + 1) % 3]
                        n += 1
                    if step[0] == "ST":
                        _, q, kb, half = step
                        u, width = q * NT + kb, T - kb * P
                        act_e.wait_ge(s_ST, at(b, N_ST, n_st + 1))
                        if u >= 2 and half == 0:
                            act_e.wait_ge(s_av, at(b, N_AV, u - 1))
                        act_e.activation(prob[:, u % 2, 2 * half:2 * half + 2, 0:width], slot[:, :, 0:width],
                                         ACT.Exp, scale=SCALE).then_inc(s_exp, 1)
                        n_st += 1
                    elif step[0] == "MT":
                        q = step[1]
                        act_e.wait_ge(s_mT, at(b, QUADS, q + 1))
                        if q:
                            act_e.wait_ge(s_mdma, at(b, 16 * QUADS, 16 * q))
                        act_e.activation(mrow[:, :], m_bf[0:12, 0:T], ACT.Copy).then_inc(s_mrow, 1)
                    elif step[0] == "AV" and step[2] == NT - 1:
                        q = step[1]
                        act_e.wait_ge(s_av, at(b, N_AV, (q + 1) * NT))
                        if q:
                            act_e.wait_ge(s_oT, at(b, QUADS, q))
                        act_e.activation(o_t[:, :], O_BANK, ACT.Copy).then_inc(s_o, 1)
                    elif step[0] == "XT" and nxt is not None:
                        xt_high(nxt, slot)
                act_e.wait_ge(s_aT, at(b, 1, 1))
                act_e.activation(ht_hi[:, :, :], ring[0][:, :, :], ACT.Copy).then_inc(s_athi, 1)

            def ffn(b, nxt):
                act_e.wait_ge(s_hT, at(b, 1, 1))
                act_e.activation(ht_hi[:, :, :], ring[0][:, :, :], ACT.Copy).then_inc(s_hthi, 1)
                act_e.wait_ge(s_logit, at(b, 1, 1))
                act_e.activation(r_sc[:, :], M_BANK[:, 0:NT * E], ACT.Sigmoid).then_inc(s_score, 1)

                def gate_up_high(u):
                    act_e.wait_ge(s_gu, at(b, UNITS, u - 1 if u >= 4 else 1))
                    act_e.activation(gu_hi[:, u % 2, :], expert(u, 0, GU_COLS), ACT.Copy).then_inc(s_guhi, 1)

                def down_high(u):
                    if u >= 4:
                        act_e.wait_ge(s_d, at(b, UNITS, u - 1))
                    act_e.activation(dn_hi[:, u % 2, :], expert(u, GU_COLS, D), ACT.Copy).then_inc(s_dnhi, 1)

                def silu_of(u):
                    act_e.wait_ge(s_gu, at(b, UNITS, u + 1))
                    if u >= 2:
                        act_e.wait_ge(s_t, at(b, UNITS, u - 1))
                    act_e.activation(silu[:, u % 2, :], ring[1 + u % 3][:, 0, :], ACT.Silu).then_inc(s_silu, 1)

                def high(u):
                    if u < SHARED:
                        act_e.wait_ge(s_t, at(b, UNITS, u + 1))
                    else:
                        act_e.wait_ge(s_a, at(b, E, u - SHARED + 1))
                    if u >= 2:
                        act_e.wait_ge(s_d, at(b, UNITS, u - 1))
                    act_e.activation(a_hi[:, u % 2, :], act[:, u % 2, :], ACT.Copy).then_inc(s_ahi, 1)

                act_e.wait_ge(s_wexp, 64)
                for u in range(UNITS):
                    silu_of(u)
                    if u >= 1:
                        high(u - 1)
                    if u == 1:
                        act_e.wait_ge(s_cwT, at(b, 1, 1))
                        act_e.activation(cw_t[:, :], ring[0][0:E, 0, :], ACT.Copy).then_inc(s_cwrow, 1)
                    if u == 0:
                        gate_up_high(SHARED)
                        gate_up_high(SHARED + 1)
                    elif 4 <= u + 2 < UNITS:
                        gate_up_high(u + 2)
                    if u - 1 >= SHARED:
                        down_high(u - 1)
                    if nxt is not None and PART_UNIT <= u < PART_UNIT + 5:
                        parts_step(nxt, u - PART_UNIT)
                high(UNITS - 1)
                down_high(UNITS - 1)

            xt_high(0, ring[0], first=True)
            project(0, first=True)
            for n in range(5):
                parts_step(0, n, first=True)
            with act_e.Fori(0, B - 1) as i:
                attend(i, i + 1)
                project(i + 1)
                ffn(i, i + 1)
            attend(B - 1, None)
            ffn(B - 1, None)

        @block.tensor
        def _(pe):
            pe.wait_ge(s_pool0, 8)
            pe.wait_ge(s_dve0, 2)

            def split_product(dst, l_hi, l_lo, r_hi, r_lo, start, stop, **kw):
                pe.matmul(dst, l_lo, r_hi, start=start, stop=False, **kw)
                pe.matmul(dst, l_hi, r_lo, start=False, stop=False, **kw)
                return pe.matmul(dst, l_hi, r_hi, start=False, stop=stop, **kw)

            def weight(tile, col, k, width, m, n):
                c = col + k * width + m
                return tile[:, c:c + n]

            def transpose_rows(slot, rows):
                for k in range(KD):
                    for t in range(NT):
                        last = pe.transpose(slot[:, k, t * P:(t + 1) * P], rows[:, t, k * P:(k + 1) * P], ident[:, :])
                return last

            def xt(b, slot):
                pe.wait_ge(s_xn, at(b, NT, NT))
                transpose_rows(slot, xn).then_inc(s_xnT, 1)

            def project(b, first=False):
                if first:
                    pe.wait_ge(s_wlo, 1)
                pe.wait_ge(s_xthi, at(b, 1, 1))
                pe.wait_ge(s_xtlo, at(b, 1, 1))
                for qk in range(2):
                    for eo in range(2):
                        m = (2 * qk + eo) * P
                        for k in range(KD):
                            last = split_product(ring[1 + qk][:, eo, :],
                                                 weight(w_hi, C_QKV, k, 3 * D, m, P), weight(w_lo, C_QKV, k, 3 * D, m, P),
                                                 xt_hi[:, k, :], xt_lo[:, k, :], k == 0, k == KD - 1)
                    last.then_inc(s_qk, 1)
                if not first:
                    pe.wait_ge(s_ln, at(b, LN_STEPS, 0) - (LN_STEPS - 3 * NT))
                for t in range(NT):
                    dst = ring[0][:, t // 2, (t % 2) * D:(t % 2 + 1) * D]
                    tok = slice(t * P, (t + 1) * P)
                    for k in range(KD):
                        last = split_product(dst, xt_hi[:, k, tok], xt_lo[:, k, tok],
                                             weight(w_hi, C_QKV, k, 3 * D, 2 * D, D),
                                             weight(w_lo, C_QKV, k, 3 * D, 2 * D, D), k == 0, k == KD - 1)
                last.then_inc(s_v, 1)

            def attend(b, nxt):
                pe.wait_ge(s_stack, at(b, N_STACK * 16, N_STACK * 16))
                n = n_s = n_st = 0
                user = [None] * 3
                user[0] = (s_y, at(b, 1, 1))
                m_user = None

                for step in PLAN:
                    kind = step[0]
                    if kind == "XT" and nxt is None:
                        n += 1
                        continue
                    if kind in ("S", "ST", "XT"):
                        r = (n + 1) % 3
                        slot = ring[r]
                        n += 1
                        if user[r] is not None:
                            pe.wait_ge(*user[r])
                    if kind == "S":
                        _, pair, qb = step
                        width, q0 = (qb + 1) * P, qb * P
                        for j in range(2):
                            h = 2 * pair + j
                            pe.matmul(slot[:, j, 0:width], q_st[0:ROWS, h, q0:q0 + P], k_st[0:ROWS, h, 0:width],
                                      start=True, stop=False)
                            last = pe.matmul(slot[:, j, q0:q0 + P], ident_b[:, :], mask_b[:, :], start=False, stop=True)
                        last.then_inc(s_S, 1)
                        n_s += 1
                        user[r] = (s_max, at(b, N_S, n_s))
                    elif kind == "ST":
                        _, q, kb, half = step
                        if kb == 0 and half == 0:
                            pe.wait_ge(s_mdma, at(b, 16 * QUADS, 16 * (q + 1)))
                        for j in range(2):
                            h = 4 * q + 2 * half + j
                            last = pe.matmul(slot[:, j, 0:T - kb * P], k_st[0:MROWS, h, kb * P:(kb + 1) * P],
                                             q_st[0:MROWS, h, kb * P:T], start=True, stop=True)
                        last.then_inc(s_ST, 1)
                        n_st += 1
                        user[r] = (s_exp, at(b, N_ST, n_st))
                    elif kind == "AV":
                        _, q, kb = step
                        u = q * NT + kb
                        pe.wait_ge(s_tri, at(b, N_AV, u + 1))
                        if kb == 0:
                            if u == 0:
                                pe.wait_ge(s_vsb, at(b, NT, NT))
                            else:
                                pe.wait_ge(s_o, at(b, QUADS, q))
                        for j in range(4):
                            last = pe.matmul(O_BANK[32 * j:32 * j + 32, kb * P:T], v_sb[:, kb, 4 * q + j, :],
                                             prob[:, u % 2, j, 0:T - kb * P], start=(kb == 0), stop=(kb == NT - 1))
                        last.then_inc(s_av, 1)
                    elif kind == "MT":
                        q = step[1]
                        pe.wait_ge(s_mp, at(b, 5 * QUADS, 5 * (q + 1)))
                        if m_user is not None:
                            pe.wait_ge(*m_user)
                        for qb in range(NT):
                            last = pe.transpose(m_bf[0:12, qb * P:(qb + 1) * P],
                                                mpart[:, qb, :, :].rearrange("p s h -> p (s h)"), ident_b[:, :])
                        last.then_inc(s_mT, 1)
                        m_user = (s_mrow, at(b, QUADS, q + 1))
                    elif kind == "OT":
                        q = step[1]
                        pe.wait_ge(s_o, at(b, QUADS, q + 1))
                        if m_user is not None:
                            pe.wait_ge(*m_user)
                        for t in range(NT):
                            last = pe.transpose(M_BANK[:, t * P:(t + 1) * P], o_t[:, t * P:(t + 1) * P], ident[:, :])
                        last.then_inc(s_oT, 1)
                        m_user = (s_att, at(b, QUADS, q + 1))
                    elif kind == "XT":
                        xt(nxt, slot)
                        user[r] = (s_xtlo, at(nxt, 1, 1))
                pe.wait_ge(s_att, at(b, QUADS, QUADS))
                pe.wait_ge(*user[0])
                transpose_rows(ring[0], att).then_inc(s_aT, 1)
                pe.wait_ge(s_athi, at(b, 1, 1))
                pe.wait_ge(s_atlo, at(b, 1, 1))
                for t in range(NT):
                    dst = ring[0][:, t // 2, (t % 2) * D:(t % 2 + 1) * D]
                    tok = slice(t * P, (t + 1) * P)
                    for k in range(KD):
                        last = split_product(dst, ht_hi[:, k, tok], ht_lo[:, k, tok],
                                             weight(w_hi, C_O, k, D, 0, D), weight(w_lo, C_O, k, D, 0, D),
                                             k == 0, k == KD - 1)
                last.then_inc(s_op, 1)

            def ffn(b, nxt):
                pe.wait_ge(s_xn2, at(b, NT, NT))
                if nxt is not None:
                    pe.wait_ge(s_vsb, at(nxt, NT, NT))
                transpose_rows(ring[0], xn2).then_inc(s_hT, 1)
                pe.wait_ge(s_hthi, at(b, 1, 1))
                pe.wait_ge(s_htlo, at(b, 1, 1))
                for t in range(NT):
                    tok = slice(t * P, (t + 1) * P)
                    dst = M_BANK[:, t * E:(t + 1) * E]
                    for k in range(KD):
                        g_hi, g_lo = weight(w_hi, C_GATE, k, E, 0, E), weight(w_lo, C_GATE, k, E, 0, E)
                        pe.matmul(dst, ht_lo[:, k, tok], g_lo, start=(k == 0), stop=False)
                        last = split_product(dst, ht_hi[:, k, tok], ht_lo[:, k, tok], g_hi, g_lo, False, k == KD - 1)
                last.then_inc(s_logit, 1)

                def gate_up(u):
                    if u < 2 and nxt is not None:
                        pe.wait_ge(s_rot, at(nxt, 8, 4 * u + 4))
                    if u == 2:
                        pe.wait_ge(s_score, at(b, 1, 1))
                    if u >= 3:
                        pe.wait_ge(s_t, at(b, UNITS, u - 2))
                    if u >= SHARED:
                        pe.wait_ge(s_gulo, at(b, E, u - SHARED + 1))
                    for n in range(2):
                        for k in range(KD):
                            if u < SHARED:
                                c = (C_SG, C_SU)[n]
                                hi, lo = weight(w_hi, c, k, D, u * P, P), weight(w_lo, c, k, D, u * P, P)
                            else:
                                c = (n * KD + k) * FI
                                hi, lo = gu_hi[:, u % 2, c:c + FI], gu_lo[:, u % 2, c:c + FI]
                            last = split_product(ring[1 + u % 3][:, n, :], hi, lo, ht_hi[:, k, :], ht_lo[:, k, :],
                                                 k == 0, k == KD - 1)
                    last.then_inc(s_gu, 1)

                def down(u):
                    if u == 0:
                        pe.wait_ge(s_cwrow, at(b, 1, 1))
                    pe.wait_ge(s_alo, at(b, UNITS, u + 1))
                    if u < SHARED:
                        hi, lo = weight(w_hi, C_SD, u, D, 0, D), weight(w_lo, C_SD, u, D, 0, D)
                    else:
                        pe.wait_ge(s_dnlo, at(b, E, u - SHARED + 1))
                        hi, lo = dn_hi[:, u % 2, :], dn_lo[:, u % 2, :]
                    for t in range(NT):
                        tok = slice(t * P, (t + 1) * P)
                        last = split_product(ring[0][:, t // 2, (t % 2) * D:(t % 2 + 1) * D],
                                             a_hi[:, u % 2, tok], a_lo[:, u % 2, tok], hi, lo,
                                             u == 0 and t % 2 == 0, u == UNITS - 1, skip_group_check=True)
                    last.then_inc(s_d, 1)

                gate_up(0)
                gate_up(1)
                pe.wait_ge(s_cw, at(b, 1, 1))
                for t in range(NT):
                    last = pe.transpose(ring[0][0:E, 0, t * P:(t + 1) * P], cw[:, t, :], ident[:, :])
                last.then_inc(s_cwT, 1)
                for u in range(UNITS):
                    if u + 2 < UNITS:
                        gate_up(u + 2)
                    down(u)

            xt(0, ring[0])
            project(0, first=True)
            with pe.Fori(0, B - 1) as i:
                attend(i, i + 1)
                project(i + 1)
                ffn(i, i + 1)
            attend(B - 1, None)
            ffn(B - 1, None)


N_STAT = 2 * NT + 1
LN_STEPS = 6 * NT
ROUTE_STEPS = 28
FLN = 4 * NT


def pack_small(w_q, w_k, w_v, w_o, gate_w, ws_g, ws_u, ws_d):
    def halves(w):
        pairs = w.reshape(H, HALF, 2, D)
        return [pairs[:, :, 0].reshape(P, D).T, pairs[:, :, 1].reshape(P, D).T]

    def tiles(wt):
        return [wt[k * P:(k + 1) * P] for k in range(KD)]

    qkv = np.concatenate(halves(w_q) + halves(w_k) + [w_v.T], axis=1)
    cols = []
    for wt in (qkv, w_o.T, ws_g.T, ws_u.T, ws_d.T, gate_w.T):
        cols += tiles(wt)
    return np.ascontiguousarray(np.concatenate(cols, axis=1))


def pack_experts(wg, wu, wd):
    cols = []
    for e in range(E):
        for w in (wg[e].T, wu[e].T):
            cols += [w[k * P:(k + 1) * P] for k in range(KD)]
        cols.append(wd[e].T)
    return np.ascontiguousarray(np.concatenate(cols, axis=1))


def rope_tables():
    inv = (np.float32(10000.0) ** (np.float32(-2.0) * np.arange(HALF, dtype=np.float32) / np.float32(DH))).astype(np.float32)
    ang = np.arange(T, dtype=np.float32)[None, :] * np.tile(inv, H)[:, None]
    return np.ascontiguousarray(np.stack([np.cos(ang), np.sin(ang)], axis=1).astype(np.float32))


def tie_tables():
    def lower(n):
        return (np.arange(n)[None, :] < np.arange(n)[:, None]).astype(np.float32).reshape(-1)

    row = np.concatenate([lower(E), lower(NG)])
    return np.ascontiguousarray(np.broadcast_to(row, (P, row.size)))


def kernel(L0_attn_x, L0_attn_W_q, L0_attn_W_k, L0_attn_W_v, L0_attn_W_o, L0_ffn_gate_w, L0_ffn_gate_bias,
           L0_ffn_Wg, L0_ffn_Wu, L0_ffn_Wd, L0_ffn_Ws_g, L0_ffn_Ws_u, L0_ffn_Ws_d):
    import concourse.bacc as bacc
    from concourse.bass_utils import run_bass_kernel_spmd

    a = np.asarray
    arrays = {
        "x": np.ascontiguousarray(a(L0_attn_x)),
        "w_small": pack_small(a(L0_attn_W_q), a(L0_attn_W_k), a(L0_attn_W_v), a(L0_attn_W_o), a(L0_ffn_gate_w),
                              a(L0_ffn_Ws_g), a(L0_ffn_Ws_u), a(L0_ffn_Ws_d)),
        "w_exp": pack_experts(a(L0_ffn_Wg), a(L0_ffn_Wu), a(L0_ffn_Wd)),
        "rope": rope_tables(),
        "ties": tie_tables(),
        "bias": np.ascontiguousarray(np.broadcast_to(a(L0_ffn_gate_bias), (P, NT, E)).reshape(P, NT * E)),
    }
    nc = bacc.Bacc("TRN2", target_bir_lowering=False, num_devices=1)
    ins = [nc.dram_tensor(n, v.shape, mybir.dt.from_np(v.dtype), kind="ExternalInput").ap() for n, v in arrays.items()]
    out = nc.dram_tensor("out", (B, T, D), mybir.dt.float32, kind="ExternalOutput").ap()
    block_kernel(nc, *ins, out)
    r = run_bass_kernel_spmd(nc, [arrays], core_ids=[0])
    return r.results[0]["out"]
```

```python
import numpy as np
import concourse.bass as bass
from concourse import mybir
from contextlib import ExitStack

B, T, D = 8, 512, 256
P = 128
NT = T // P
KD = D // P
H, DH = 16, 16
HALF = DH // 2
QUADS, PAIRS = H // 4, H // 2
E, FI, TOPK, NG = 16, 128, 4, 4
EPG = E // NG
SHARED = 2
UNITS = SHARED + E
EPS = 1e-5
ROUTE_SCALE = 2.5
SCALE = DH ** -0.5
MASKED = -1e38
BIG = 1e30
MARK = 1e38
ABSENT = 3e38

Q_PART = [0, 0, 0, 1, 1, 2]
K_PART = [0, 1, 2, 0, 1, 0]
SLOTS = len(Q_PART)
ROWS = SLOTS * DH
MROWS = ROWS + 3

C_QKV = 0
C_O = C_QKV + KD * 3 * D
C_SG = C_O + KD * D
C_SU = C_SG + KD * D
C_SD = C_SU + KD * D
C_GATE = C_SD + KD * D
C_ALL = C_GATE + KD * E
GU_COLS = KD * FI * 2
EXP_COLS = GU_COLS + D

ROT = [(0, 1, 2, 3), (4, 5, 1, 3)]
SUM = [0, 2, 4, 1]
SPARE = [3, 5]
PART_UNIT = 2
HEAD_UNIT = 10

GU_SLOT = [(3, 1, 2)[u % 3] if u < HEAD_UNIT else (1, 2)[(u - HEAD_UNIT) % 2] for u in range(UNITS)]

N_S = PAIRS * NT
N_ST = QUADS * NT * 2
N_AV = QUADS * NT
N_STACK = 2 * 2 * SLOTS


S_UNITS = [(pair, qb) for pair in range(PAIRS) for qb in range(NT)]
HEAD_S = 2 * 2 * NT
HEAD = [("S", n) for n in range(HEAD_S)]
HEAD.insert(2 * NT + 2, ("MT", 0))
HEAD_SLOT = [3 if i < 2 * (UNITS - 2 - HEAD_UNIT) else (1, 2, 3)[i % 3] for i in range(len(HEAD))]


def last_head(slot, before=len(HEAD)):
    return max((i for i in range(before) if HEAD_SLOT[i] == slot), default=None)


def head_steps(u):
    n = 2 * (u - HEAD_UNIT)
    return [HEAD[i] if 0 <= i < len(HEAD) else None for i in (n, n + 1)]


HEAD_LEFT = HEAD[2 * (UNITS - HEAD_UNIT):]


SPLIT_UNIT = 16
SPLIT_STEP = (5, 9)
FINAL_STEP = 2
NORM_STEP = 5
AV_LAG = 1
S_FROM = 1
FLN_AFTER = (1, 3)
LN_AFTER = (4, 6)
AT_AFTER = 10
MT_AFTER = (1, 5, 9)


def attention_plan():
    plan = []
    s_rest = [("S", n) for n in range(HEAD_S, N_S)]
    for u in range(N_AV):
        plan.append(("ST", u // NT, u % NT, 0))
        if s_rest and u >= S_FROM:
            plan.append(s_rest.pop(0))
        plan.append(("ST", u // NT, u % NT, 1))
        if u >= AV_LAG:
            v = u - AV_LAG
            plan.append(("AV", v // NT, v % NT))
            if v % NT == 0 and v:
                plan.append(("OT", v // NT - 1))
        if s_rest and u >= S_FROM:
            plan.append(s_rest.pop(0))
        for q, after in enumerate(MT_AFTER):
            if u == after:
                plan.append(("MT", q + 1))
        if u == AT_AFTER:
            plan.append(("AT",))
        if u in FLN_AFTER:
            plan.append(("FLN", FLN_AFTER.index(u)))
        if u in LN_AFTER:
            plan.append(("LN", LN_AFTER.index(u)))
    plan += [("AV", QUADS - 1, NT - 1), ("XT",), ("OT", QUADS - 1)]
    return plan


PLAN = attention_plan()


def block_kernel(nc, x, w_small, w_exp, rope, ties, bias, out):
    fp32, fp32r, bf16 = mybir.dt.float32, mybir.dt.float32r, mybir.dt.bfloat16
    ALU, ACT, AX = mybir.AluOpType, mybir.ActivationFunctionType, mybir.AxisListType

    ctx = ExitStack()
    with ctx:
        def sb(name, shape, dt=fp32):
            return ctx.enter_context(nc.sbuf_tensor(name, shape, dt))

        def sem(name):
            return ctx.enter_context(nc.semaphore(name))

        part_dram = nc.dram_tensor("part_scratch", (4, P, 3, T), bf16, kind="Internal").ap()
        cw_dram = nc.dram_tensor("cw_scratch", (E, T), fp32, kind="Internal").ap()

        w_hi = sb("w_hi", [P, C_ALL], fp32r)
        w_lo = sb("w_lo", [P, C_ALL], fp32r)
        w_raw = sb("w_raw", [P, E * EXP_COLS])
        gu_hi = sb("gu_hi", [P, 2, 2 * KD * FI], fp32r)
        gu_lo = sb("gu_lo", [P, 2, 2 * KD * FI], fp32r)
        dn_hi = sb("dn_hi", [P, 2, D], fp32r)
        dn_lo = sb("dn_lo", [P, 2, D], fp32r)
        rope_t = sb("rope_t", [P, 2, T])
        tie_t = sb("tie_t", [P, NG * NG])
        bias_t = sb("bias_t", [P, NT * E])
        ident = sb("ident", [P, P])
        ident_b = sb("ident_b", [P, P], bf16)
        mask_b = sb("mask_b", [P, P], bf16)
        minus_half = sb("minus_half", [P, NT])
        x_ln = sb("x_ln", [P, NT, D])
        xn = x_ln
        st1 = sb("st1", [P, NT, 6])
        mv1 = sb("mv1", [P, NT, 2])
        ve1 = sb("ve1", [P, NT])
        rstd1 = sb("rstd1", [P, NT])
        xt_hi = sb("xt_hi", [P, KD, T], fp32r)
        xt_lo = sb("xt_lo", [P, KD, T], fp32r)
        rot = sb("rot", [P, 6, T])
        part = sb("part", [P, 2, 2, 3, T], bf16)
        q_st = sb("q_st", [P, H, T], bf16)
        k_st = sb("k_st", [P, H, T], bf16)
        v_sb = sb("v_sb", [P, NT, H, 32])
        nmax = sb("nmax", [P, NT, H])
        mres = sb("mres", [P, 2, NT, 4])
        mpart = sb("mpart", [P, NT, 3, 4], bf16)
        mrow = rot[:, 5, :].bitcast(bf16)[0:12, 0:T]
        prob = sb("prob", [P, 2, 4, T])
        mask_f = prob[:, 0, 0, 0:P]
        o_t = sb("o_t", [P, T])
        rden = sb("rden", [P, NT, 4])
        ht_hi = sb("ht_hi", [P, KD, T], fp32r)
        ht_lo = sb("ht_lo", [P, KD, T], fp32r)
        x1 = sb("x1", [P, NT, D])
        xn2 = sb("xn2", [P, NT, D])
        att = rot[:, 0:2, :].rearrange("p a (c d) -> p (a c) d", d=D)
        st2 = sb("st2", [P, NT, 6])
        mv2 = sb("mv2", [P, NT, 2])
        ve2 = sb("ve2", [P, NT])
        rstd2 = sb("rstd2", [P, NT])
        r_sc = sb("r_sc", [P, NT * E])
        r_sf = sb("r_sf", [P, NT * E])
        r_hi = sb("r_hi", [P, NT * NG, 2])
        r_lo = sb("r_lo", [P, NT * NG, 2])
        r_g = sb("r_g", [P, 5, NT * NG])
        r_b = prob[:, 0, 0, 0:NT * NG * NG]
        r_c = prob[:, 0, 1, 0:NT * NG * NG]
        r_top = sb("r_top", [P, NT, 8])
        r_d = prob[:, 0, 2:4, 0:NT * E]
        cw = sb("cw", [P, NT, E])
        r_s = sb("r_s", [P, 3, NT])
        cw_t = o_t[0:E, :]
        sc_t = o_t[0:E, :]
        cwb, silu, act = prob[:, 0, :, :], prob[:, 1, 0:2, :], prob[:, 1, 2:4, :]
        a_hi, a_lo = xt_hi, xt_lo
        stage = q_st[:, :, :].rearrange("p h n -> p (h n)").bitcast(fp32)[:, 0:C_ALL]

        ring = [ctx.enter_context(nc.psum_tensor(f"ring{i}", [P, 2, T], fp32)) for i in range(4)]
        O_BANK, M_BANK = ring[3][:, 0, :], ring[3][:, 1, :]
        m_bf = M_BANK.bitcast(bf16)

        s_qkvin = sem("qkv_loaded")
        s_small = sem("small_loaded")
        s_const = sem("constants_loaded")
        s_wexp = sem("experts_loaded")
        s_pool0 = sem("pool_constants")
        s_dve0 = sem("dve_constants")
        s_whi = sem("weights_high")
        s_wlo = sem("weights_low")
        s_seen_dve = sem("waited_dve")
        s_seen_pool = sem("waited_pool")
        s_x = sem("x_loaded")
        s_stat1 = sem("stats1")
        s_pow1 = sem("rstd1_ready")
        s_xn = sem("xn_ready")
        s_xnT = sem("xn_transposed")
        s_xthi = sem("xt_high")
        s_xtlo = sem("xt_low")
        s_qk = sem("qk_products")
        s_v = sem("v_products")
        s_vsb = sem("v_copied")
        s_rot = sem("rotary_products")
        s_sum = sem("rotary_sums")
        s_phi = sem("part_high")
        s_pres = sem("part_residual")
        s_pmid = sem("part_middle")
        s_plo = sem("part_low")
        s_pout = [sem(f"parts_stored{n}") for n in range(4)]
        s_stack = sem("stacked")
        s_S = sem("scores")
        s_max = sem("row_maxima")
        s_mp = sem("maxima_split")
        s_mT = sem("maxima_transposed")
        s_mrow = sem("maxima_rows")
        s_mdma = sem("maxima_stacked")
        s_ST = sem("scores_transposed")
        s_exp = sem("exponentials")
        s_tri = sem("diagonal_cut")
        s_av = sem("pv_step")
        s_o = sem("o_copied")
        s_oT = sem("o_transposed")
        s_rden = sem("denominators")
        s_att = sem("attention_rows")
        s_aT = sem("attention_transposed")
        s_athi = sem("at_high")
        s_atlo = sem("at_low")
        s_op = sem("o_projected")
        s_x1in = sem("x1_loaded")
        s_ln = sem("ln_steps")
        s_lnv = sem("ln_variance")
        s_lnr = sem("ln_rstd")
        s_xn2 = sem("xn2_ready")
        s_hT = sem("xn2_transposed")
        s_hthi = sem("ht_high")
        s_htlo = sem("ht_low")
        s_logit = sem("logits")
        s_score = sem("router_scores")
        s_scT = sem("router_scores_transposed")
        s_route = sem("router_steps")
        s_cw = sem("gates_ready")
        s_cwT = sem("gates_transposed")
        s_cwrow = sem("gates_rows")
        s_cwout = sem("gates_stored")
        s_cwb = [sem(f"gates_broadcast{i}") for i in range(4)]
        s_guhi = sem("gate_up_weights_high")
        s_gulo = sem("gate_up_weights_low")
        s_dnhi = sem("down_weights_high")
        s_dnlo = sem("down_weights_low")
        s_gu = sem("gate_up")
        s_silu = sem("silu")
        s_t = sem("silu_times_up")
        s_a = sem("gated")
        s_ahi = sem("act_high")
        s_alo = sem("act_low")
        s_d = sem("down")
        s_y = sem("y_read")
        s_fln = sem("final_ln_steps")
        s_fv = sem("final_variance")
        s_fr = sem("final_rstd")
        s_final = sem("output_rows")
        s_out = sem("out_stored")

        def at(b, per_seq, n):
            return b * per_seq + n

        def seq(b):
            return bass.ds(b, 1) if not isinstance(b, int) else slice(b, b + 1)

        def expert(u, col, n):
            c = (u - SHARED) * EXP_COLS + col
            return w_raw[:, c:c + n]

        block = ctx.enter_context(nc.Block())

        @block.sync
        def _(sp):
            def load_x(b):
                sp.dma_start(x_ln[:, :, :], x[seq(b)].rearrange("a (t p) d -> p (a t) d", p=P)).then_inc(s_x, 16)

            def load_x1(b):
                sp.dma_start(x1[:, :, :], x[seq(b)].rearrange("a (t p) d -> p (a t) d", p=P)).then_inc(s_x1in, 16)

            def store_parts(b, n):
                sp.wait_ge(s_plo, at(b, 4, n + 1))
                sp.dma_start(part_dram[n], part[:, n // 2, n % 2, :, :]).then_inc(s_pout[n], 16)

            def stack(b, n):
                dst, parts = ((q_st, Q_PART), (k_st, K_PART))[n // 2]
                sp.wait_ge(s_pout[n], at(b, 16, 16))
                for s in range(SLOTS):
                    r = s * DH + (n % 2) * HALF
                    by_pair = part_dram[n, :, parts[s], :].rearrange("(h j) t -> j h t", j=HALF)
                    sp.dma_start(dst[r:r + HALF, :, :], by_pair).then_inc(s_stack, 16)

            def ffn(b, nxt):
                sp.wait_ge(s_cwrow, at(b, 1, 1))
                sp.dma_start(cw_dram, cw_t[:, :]).then_inc(s_cwout, 16)
                sp.wait_ge(s_cwout, at(b, 16, 16))
                for e in range(E):
                    if nxt is not None and 4 <= e < 8:
                        store_parts(nxt, e - 4)
                    if nxt is not None and 6 <= e < 10:
                        if e == 6:
                            sp.wait_ge(s_ST, nxt * N_ST)
                        stack(nxt, e - 6)
                    if e >= 4:
                        sp.wait_ge(s_a, at(b, E, e - 3))
                    sp.dma_start(cwb[:, e % 4, :], cw_dram[e:e + 1, :].to_broadcast([P, T])).then_inc(s_cwb[e % 4], 16)

            def store(b):
                sp.wait_ge(s_final, at(b, NT, NT))
                sp.dma_start(out[seq(b)].rearrange("a (t p) d -> p (a t) d", p=P), xn2[:, :, :]).then_inc(s_out, 16)
                sp.wait_ge(s_out, at(b, 16, 16))

            load_x(0)
            sp.dma_start(stage[:, 0:C_O], w_small[:, 0:C_O]).then_inc(s_qkvin, 16)
            sp.dma_start(stage[:, C_O:], w_small[:, C_O:]).then_inc(s_small, 16)
            sp.dma_start(rope_t[:, :, :], rope).then_inc(s_const, 16)
            sp.dma_start(tie_t[:, :], ties).then_inc(s_const, 16)
            sp.dma_start(bias_t[:, :], bias).then_inc(s_const, 16)
            sp.wait_ge(s_wlo, 2)
            for n in range(4):
                store_parts(0, n)
            for n in range(4):
                stack(0, n)
            load_x1(0)
            for e in range(0, E, 4):
                sp.dma_start(w_raw[:, e * EXP_COLS:(e + 4) * EXP_COLS], w_exp[:, e * EXP_COLS:(e + 4) * EXP_COLS]
                             ).then_inc(s_wexp, 16)
            with sp.Fori(0, B - 1) as i:
                ffn(i, i + 1)
                store(i)
                load_x1(i + 1)
            ffn(B - 1, None)
            store(B - 1)

        @block.gpsimd
        def _(pool):
            pool.memset(ident[:, :], 0.0).then_inc(s_pool0, 1)
            pool.memset(mask_f, 0.0).then_inc(s_pool0, 1)
            pool.memset(minus_half[:, :], -0.5).then_inc(s_pool0, 1)
            pool.memset(v_sb[:, :, :, :], 0.0).then_inc(s_pool0, 1)
            pool.memset(k_st[:, :, :], 1.0).then_inc(s_pool0, 1)
            pool.wait_ge(s_pool0, 5)
            pool.affine_select(out=ident[:, :], in_=ident[:, :], compare_op=ALU.not_equal, fill=1.0,
                               base=0, pattern=[[-1, P]], channel_multiplier=1).then_inc(s_pool0, 1)
            pool.affine_select(out=mask_f, in_=mask_f, compare_op=ALU.is_ge, fill=MASKED,
                               base=0, pattern=[[-1, P]], channel_multiplier=1).then_inc(s_pool0, 1)
            pool.memset(v_sb[:, :, :, DH:DH + 1], 1.0).then_inc(s_pool0, 1)

            def norm(b):
                pool.wait_ge(s_stat1, at(b, N_STAT, N_STAT))
                pool.tensor_tensor(rstd1[:, :], ve1[:, :], minus_half[:, :], ALU.pow).then_inc(s_pow1, 1)

            def project(b):
                for qk in range(2):
                    ec, os, es, oc = ROT[qk]
                    pool.wait_ge(s_rot, at(b, 8, 4 * qk + 2))
                    pool.tensor_tensor(rot[:, ec, :], rot[:, ec, :], rot[:, os, :], ALU.subtract).then_inc(s_sum, 1)
                    pool.wait_ge(s_rot, at(b, 8, 4 * qk + 4))
                    pool.tensor_tensor(rot[:, es, :], rot[:, es, :], rot[:, oc, :], ALU.add).then_inc(s_sum, 1)

            def split_max(b, q):
                full = nmax[:, :, 4 * q:4 * q + 4]
                pool.wait_ge(s_max, at(b, N_S, (2 * q + 2) * NT))
                if q:
                    pool.wait_ge(s_mT, at(b, QUADS, q))
                base = 5 * q
                pool.sem_inc(s_seen_pool, 1)
                pool.tensor_copy(mpart[:, :, 0, :], full).then_inc(s_mp, 1)
                pool.wait_ge(s_mp, at(b, 5 * QUADS, base + 1))
                pool.tensor_tensor(mres[:, 0, :, :], full, mpart[:, :, 0, :], ALU.subtract).then_inc(s_mp, 1)
                pool.wait_ge(s_mp, at(b, 5 * QUADS, base + 2))
                pool.sem_inc(s_seen_pool, 1)
                pool.tensor_copy(mpart[:, :, 1, :], mres[:, 0, :, :]).then_inc(s_mp, 1)
                pool.wait_ge(s_mp, at(b, 5 * QUADS, base + 3))
                pool.tensor_tensor(mres[:, 1, :, :], mres[:, 0, :, :], mpart[:, :, 1, :],
                                  ALU.subtract).then_inc(s_mp, 1)
                pool.wait_ge(s_mp, at(b, 5 * QUADS, base + 4))
                pool.sem_inc(s_seen_pool, 1)
                pool.tensor_copy(mpart[:, :, 2, :], mres[:, 1, :, :]).then_inc(s_mp, 1)

            def final_rstd(b):
                pool.wait_ge(s_fv, at(b, 1, 1))
                pool.tensor_tensor(rstd2[:, :], ve2[:, :], minus_half[:, :], ALU.pow).then_inc(s_fr, 1)

            def output_rows(b, t):
                pool.wait_ge(s_fln, at(b, FLN, 2 * NT + t + 1))
                pool.tensor_tensor(xn2[:, t, :], xn2[:, t, :], x1[:, t, :], ALU.add).then_inc(s_final, 1)

            def attend(b, nxt, prev):
                for u in range(N_AV):
                    if u in SPLIT_STEP:
                        split_max(b, 2 + SPLIT_STEP.index(u))
                    if prev is not None and u == FINAL_STEP:
                        final_rstd(prev)
                    if prev is not None and 0 < u - FINAL_STEP <= NT:
                        output_rows(prev, u - FINAL_STEP - 1)
                    if u == NORM_STEP and nxt is not None:
                        norm(nxt)
                    for half in range(2):
                        pool.wait_ge(s_exp, at(b, N_ST, 2 * u + half + 1))
                        pool.sem_inc(s_seen_pool, 1)
                        diag = prob[:, u % 2, 2 * half:2 * half + 2, 0:P]
                        pool.affine_select(out=diag, in_=diag, compare_op=ALU.is_ge, fill=0.0, base=0,
                                           pattern=[[0, 2], [1, P]], channel_multiplier=-1).then_inc(s_tri, 1)
                for n in range(4):
                    half = slice(n % 2 * HT, (n % 2 + 1) * HT)
                    pool.wait_ge(s_lnv, at(b, 4, n + 1))
                    pool.tensor_tensor(rstd2[:, half], ve2[:, half], minus_half[:, half], ALU.pow).then_inc(s_lnr, 1)

            def ffn(b, nxt):
                def gate_up_low(u):
                    pool.wait_ge(s_guhi, at(b, E, u - SHARED + 1))
                    pool.tensor_tensor(gu_lo[:, u % 2, :], expert(u, 0, GU_COLS), gu_hi[:, u % 2, :],
                                       ALU.subtract).then_inc(s_gulo, 1)

                def down_low(u):
                    pool.wait_ge(s_dnhi, at(b, E, u - SHARED + 1))
                    pool.tensor_tensor(dn_lo[:, u % 2, :], expert(u, GU_COLS, D), dn_hi[:, u % 2, :],
                                       ALU.subtract).then_inc(s_dnlo, 1)

                for u in range(UNITS + 1):
                    for v in ((SHARED, SHARED + 1) if u == 0 else (u + 2,)):
                        if SHARED <= v < UNITS and not (u == 1 and v == 3):
                            gate_up_low(v)
                    if u - 1 >= SHARED:
                        down_low(u - 1)
                    if nxt is not None and u == SPLIT_UNIT:
                        split_max(nxt, 0)
                if nxt is not None:
                    split_max(nxt, 1)

            norm(0)
            project(0)
            split_max(0, 0)
            split_max(0, 1)
            attend(0, 1, None)
            project(1)
            with pool.Fori(0, B - 2) as i:
                ffn(i, i + 1)
                attend(i + 1, i + 2, i)
                project(i + 2)
            ffn(B - 2, B - 1)
            attend(B - 1, None, B - 2)
            ffn(B - 1, None)
            final_rstd(B - 1)
            for t in range(NT):
                output_rows(B - 1, t)

        @block.vector
        def _(dve):
            dve.wait_ge(s_pool0, 8)
            dve.tensor_copy(ident_b[:, :], ident[:, :]).then_inc(s_dve0, 1)
            dve.tensor_copy(mask_b[:, :], mask_f).then_inc(s_dve0, 1)

            def weights_low(n, cols):
                dve.wait_ge(s_whi, n + 1)
                dve.tensor_tensor(w_lo[:, cols], stage[:, cols], w_hi[:, cols], ALU.subtract).then_inc(s_wlo, 1)

            def norm_statistics(b):
                dve.wait_ge(s_x, at(b, 16, 16))
                for t in range(NT):
                    dve.bn_stats(st1[:, t, :], x_ln[:, t, :]).then_inc(s_stat1, 1)
                for t in range(NT):
                    dve.wait_ge(s_stat1, at(b, N_STAT, t + 1))
                    dve.sem_inc(s_seen_dve, 1)
                    dve.bn_aggr(mv1[:, t, :], st1[:, t, :]).then_inc(s_stat1, 1)
                dve.wait_ge(s_stat1, at(b, N_STAT, 2 * NT))
                dve.tensor_scalar(ve1[:, :], mv1[:, :, 1], EPS, None, ALU.add).then_inc(s_stat1, 1)

            def norm_rows(b):
                dve.wait_ge(s_pow1, at(b, 1, 1))
                for t in range(NT):
                    dve.tensor_scalar(xn[:, t, :], x_ln[:, t, :], mv1[:, t, 0:1], rstd1[:, t:t + 1],
                                      ALU.subtract, ALU.mult).then_inc(s_xn, 1)

            def xt_low(b, slot):
                dve.wait_ge(s_xthi, at(b, 1, 1))
                dve.tensor_tensor(xt_lo[:, :, :], slot[:, :, :], xt_hi[:, :, :], ALU.subtract).then_inc(s_xtlo, 1)

            def project(b, first=False):
                if first:
                    dve.wait_ge(s_const, 48)
                cos, sin = rope_t[:, 0, :], rope_t[:, 1, :]
                for qk in range(2):
                    dve.wait_ge(s_qk, at(b, 2, qk + 1))
                    even, odd = ring[1 + qk][:, 0, :], ring[1 + qk][:, 1, :]
                    for n, (src, tab) in enumerate(((even, cos), (odd, sin), (even, sin), (odd, cos))):
                        if qk and n >= 2:
                            dve.wait_ge(s_sum, at(b, 4, n - 1))
                        dve.tensor_tensor(rot[:, ROT[qk][n], :], src, tab, ALU.mult).then_inc(s_rot, 1)

            def part_residual(b, n):
                dve.wait_ge(s_phi, at(b, 4, n + 1))
                if n == 0:
                    dve.wait_ge(s_sum, at(b, 4, 4))
                if n >= 2:
                    dve.wait_ge(s_plo, at(b, 4, n - 1))
                dve.tensor_tensor(rot[:, SPARE[n % 2], :], rot[:, SUM[n], :], part[:, n // 2, n % 2, 0, :],
                                  ALU.subtract).then_inc(s_pres, 1)

            def part_low(b, n):
                dve.wait_ge(s_pmid, at(b, 4, n + 1))
                dve.tensor_tensor(part[:, n // 2, n % 2, 2, :], rot[:, SPARE[n % 2], :], part[:, n // 2, n % 2, 1, :],
                                  ALU.subtract).then_inc(s_plo, 1)

            def parts_step(b, n):
                if n < 4:
                    part_residual(b, n)
                if n >= 1:
                    part_low(b, n - 1)

            def row_max(b, n_s, slot):
                dve.wait_ge(s_S, at(b, N_S, n_s + 1))
                pair, qb = S_UNITS[n_s]
                n = (qb + 1) * P
                dve.tensor_reduce(nmax[:, qb, 2 * pair:2 * pair + 2], slot[:, :, 0:n], AX.X, ALU.max,
                                  negate=True).then_inc(s_max, 1)

            def head_rows(b, q):
                o = M_BANK.rearrange("p (t h c) -> p t h c", t=NT, h=4)
                dve.wait_ge(s_oT, at(b, QUADS, q + 1))
                dve.reciprocal(rden[:, :, :], o[:, :, :, DH]).then_inc(s_rden, 1)
                dve.wait_ge(s_rden, at(b, QUADS, q + 1))
                dst = att[:, :, :].rearrange("p t (h c) -> p t h c", c=DH)[:, :, 4 * q:4 * q + 4, :]
                dve.tensor_tensor(dst, o[:, :, :, 0:DH], rden[:, :, :].unsqueeze(3).to_broadcast([P, NT, 4, DH]),
                                  ALU.mult).then_inc(s_att, 1)

            def ht_low(b, k, src, high_sem, low_sem):
                dve.wait_ge(high_sem, at(b, KD, k + 1))
                dve.tensor_tensor(ht_lo[:, k, :], src, ht_hi[:, k, :], ALU.subtract).then_inc(low_sem, 1)

            def statistics(src, step, value, v_sem, total, b, tiles=range(NT)):
                for t in tiles:
                    dve.bn_stats(st2[:, t, :], src(t)).then_inc(step, 1)
                for i, t in enumerate(tiles):
                    dve.wait_ge(step, at(b, total, value + i + 1))
                    dve.sem_inc(s_seen_dve, 1)
                    dve.bn_aggr(mv2[:, t, :], st2[:, t, :]).then_inc(step, 1)
                dve.wait_ge(step, at(b, total, value + 2 * len(tiles)))
                span = slice(tiles[0], tiles[-1] + 1)
                dve.tensor_scalar(ve2[:, span], mv2[:, span, 1], EPS, None, ALU.add).then_inc(v_sem, 1)

            def head(b, step):
                if step is not None and step[0] == "S":
                    row_max(b, step[1], ring[HEAD_SLOT[HEAD.index(step)]])

            def final_statistics(b):
                dve.wait_ge(s_y, at(b, 1, 2))
                statistics(lambda t: xn2[:, t, :], s_fln, 0, s_fv, FLN, b)

            def final_rows(b):
                dve.wait_ge(s_fr, at(b, 1, 1))
                for t in range(NT):
                    dve.tensor_scalar(xn2[:, t, :], xn2[:, t, :], mv2[:, t, 0:1], rstd2[:, t:t + 1],
                                      ALU.subtract, ALU.mult).then_inc(s_fln, 1)

            def attend(b, nxt, prev):
                n = 0
                for step in PLAN:
                    if step[0] in ("S", "ST"):
                        slot = ring[n % 3]
                        n += 1
                    if step[0] == "S":
                        row_max(b, step[1], slot)
                    elif step[0] == "OT":
                        head_rows(b, step[1])
                    elif step[0] == "AT":
                        ht_low(b, 0, M_BANK, s_athi, s_atlo)
                    elif step[0] == "LN" and nxt is not None:
                        (norm_statistics, norm_rows)[step[1]](nxt)
                    elif step[0] == "FLN" and prev is not None:
                        (final_statistics, final_rows)[step[1]](prev)
                if nxt is not None:
                    xt_low(nxt, ring[1])
                ht_low(b, 1, ring[0][:, 1, :], s_athi, s_atlo)
                proj = ring[0][:, :, :].rearrange("p a (c d) -> p (a c) d", d=D)
                for h in range(2):
                    dve.wait_ge(s_op, at(b, 2, h + 1))
                    statistics(lambda t: proj[:, t, :], s_ln, 2 * HT * h, s_lnv, LN_STEPS, b, HALVES[h])
                for h in range(2):
                    done = 2 * NT + 4 * HT * h
                    dve.wait_ge(s_lnr, at(b, 4, h + 1))
                    if h == 0:
                        dve.wait_ge(s_x1in, at(b, 16, 16))
                    for t in HALVES[h]:
                        dve.tensor_scalar(xn2[:, t, :], proj[:, t, :], mv2[:, t, 0:1], rstd2[:, t:t + 1],
                                          ALU.subtract, ALU.mult).then_inc(s_ln, 1)
                    for i, t in enumerate(HALVES[h]):
                        dve.wait_ge(s_ln, at(b, LN_STEPS, done + i + 1))
                        dve.tensor_tensor(x1[:, t, :], x1[:, t, :], xn2[:, t, :], ALU.add).then_inc(s_ln, 1)
                    dve.wait_ge(s_ln, at(b, LN_STEPS, done + 2 * HT))
                    statistics(lambda t: x1[:, t, :], s_ln, done + 2 * HT, s_lnv, LN_STEPS, b, HALVES[h])
                for h in range(2):
                    dve.wait_ge(s_lnr, at(b, 4, h + 3))
                    for t in HALVES[h]:
                        dve.tensor_scalar(xn2[:, t, :], x1[:, t, :], mv2[:, t, 0:1], rstd2[:, t:t + 1],
                                          ALU.subtract, ALU.mult).then_inc(s_xn2, 1)

            def route(b):
                count = [0]

                def step(ins):
                    count[0] += 1
                    ins.then_inc(s_route, 1)
                    dve.wait_ge(s_route, at(b, ROUTE_STEPS, count[0]))

                def beaten(rank, v, n, tie, wide_a, wide_b):
                    other = v.unsqueeze(2).to_broadcast([P, NT, n, n])
                    own = v.unsqueeze(3).to_broadcast([P, NT, n, n])
                    a = wide_a[:, 0:NT * n * n].rearrange("p (t g k) -> p t g k", t=NT, g=n)
                    c = wide_b[:, 0:NT * n * n].rearrange("p (t g k) -> p t g k", t=NT, g=n)
                    tb = tie.rearrange("p (g k) -> p g k", g=n).unsqueeze(1).to_broadcast([P, NT, n, n])
                    step(dve.tensor_tensor(a, other, own, ALU.is_equal))
                    step(dve.tensor_tensor(a, a, tb, ALU.mult))
                    step(dve.tensor_tensor(c, other, own, ALU.is_gt))
                    step(dve.tensor_tensor(a, a, c, ALU.add))
                    step(dve.tensor_reduce(rank, a, AX.X, ALU.add))

                t_e = lambda ap: ap.rearrange("p (t e) -> p t e", t=NT)
                t_g = lambda ap: ap.rearrange("p (t g) -> p t g", t=NT)
                grouped = lambda ap: ap.rearrange("p (g k) -> p g k", k=EPG)
                dve.wait_ge(s_scT, at(b, 1, 1))
                step(dve.tensor_copy(r_sc[:, :], ring[0][:, 1, 0:NT * E]))
                step(dve.tensor_tensor(r_sf[:, :], r_sc[:, :], bias_t[:, :], ALU.add))
                quad = grouped(r_sf[:, :]).rearrange("p g (a c) -> p g a c", a=2)
                step(dve.tensor_tensor(r_hi[:, :, :], quad[:, :, :, 0], quad[:, :, :, 1], ALU.max))
                step(dve.tensor_tensor(r_lo[:, :, :], quad[:, :, :, 0], quad[:, :, :, 1], ALU.min))
                step(dve.tensor_tensor(r_g[:, 0, :], r_hi[:, :, 0], r_hi[:, :, 1], ALU.max))
                step(dve.tensor_tensor(r_g[:, 1, :], r_hi[:, :, 0], r_hi[:, :, 1], ALU.min))
                step(dve.tensor_tensor(r_g[:, 2, :], r_lo[:, :, 0], r_lo[:, :, 1], ALU.max))
                step(dve.tensor_tensor(r_g[:, 1, :], r_g[:, 1, :], r_g[:, 2, :], ALU.max))
                step(dve.tensor_tensor(r_g[:, 0, :], r_g[:, 0, :], r_g[:, 1, :], ALU.add))
                beaten(t_g(r_g[:, 3, :]), t_g(r_g[:, 0, :]), NG, tie_t[:, :], r_b, r_c)
                step(dve.tensor_scalar(r_g[:, 4, :], r_g[:, 3, :], 1.5, -BIG, ALU.is_gt, ALU.mult))
                step(dve.tensor_tensor(grouped(r_sf[:, :]), grouped(r_sf[:, :]),
                                       r_g[:, 4, :].unsqueeze(2).to_broadcast([P, NT * NG, EPG]), ALU.add))
                dve.sem_inc(s_seen_dve, 1)
                for t in range(NT):
                    dve.max(r_top[:, t, :], r_sf[:, t * E:(t + 1) * E]).then_inc(s_route, 1)
                count[0] += NT
                dve.wait_ge(s_route, at(b, ROUTE_STEPS, count[0]))
                dve.sem_inc(s_seen_dve, 1)
                step(dve.memset(r_top[:, :, TOPK:], ABSENT))
                dve.sem_inc(s_seen_dve, 1)
                for t in range(NT):
                    dve.match_replace(r_d[:, 0, t * E:(t + 1) * E], r_top[:, t, :], r_sf[:, t * E:(t + 1) * E],
                                      MARK).then_inc(s_route, 1)
                count[0] += NT
                dve.wait_ge(s_route, at(b, ROUTE_STEPS, count[0]))
                step(dve.tensor_scalar(r_d[:, 0, :], r_d[:, 0, :], MARK / 2, None, ALU.is_gt))
                step(dve.tensor_tensor(r_d[:, 1, :], r_d[:, 0, :], r_sc[:, :], ALU.mult))
                step(dve.tensor_reduce(r_s[:, 0, :], t_e(r_d[:, 1, :]), AX.X, ALU.add))
                step(dve.tensor_scalar(r_s[:, 1, :], r_s[:, 0, :], 1e-20, None, ALU.add))
                step(dve.reciprocal(r_s[:, 2, :], r_s[:, 1, :]))
                step(dve.tensor_tensor(t_e(r_d[:, 1, :]), t_e(r_d[:, 1, :]),
                                       r_s[:, 2, :].unsqueeze(2).to_broadcast([P, NT, E]), ALU.mult))
                assert count[0] == ROUTE_STEPS
                dve.tensor_scalar(cw[:, :, :], t_e(r_d[:, 1, :]), ROUTE_SCALE, None, ALU.mult).then_inc(s_cw, 1)

            def ffn(b, nxt):
                for k in range(KD):
                    ht_low(b, k, ring[0][:, k, :], s_hthi, s_htlo)
                if nxt is not None:
                    project(nxt)
                route(b)

                def low(u):
                    dve.wait_ge(s_ahi, at(b, UNITS, u + 1))
                    dve.tensor_tensor(a_lo[:, u % 2, :], act[:, u % 2, :], a_hi[:, u % 2, :],
                                      ALU.subtract).then_inc(s_alo, 1)

                for u in range(UNITS + 2):
                    before, after = head_steps(u - 2) if nxt is not None else (None, None)
                    if u < UNITS:
                        head(nxt, before)
                        if u >= 2:
                            dve.wait_ge(s_alo, at(b, UNITS, u - 1))
                        dve.wait_ge(s_silu, at(b, UNITS, u + 1))
                        dve.tensor_tensor(act[:, u % 2, :], silu[:, u % 2, :], ring[GU_SLOT[u]][:, 1, :],
                                          ALU.mult).then_inc(s_t, 1)
                    if 1 <= u <= UNITS:
                        low(u - 1)
                    if u >= UNITS:
                        head(nxt, before)
                    if SHARED <= u < UNITS:
                        e = u - SHARED
                        dve.wait_ge(s_t, at(b, UNITS, u + 1))
                        dve.wait_ge(s_cwb[e % 4], at(b, 16 * (E // 4), 16 * (e // 4 + 1)))
                        dve.tensor_tensor(act[:, u % 2, :], act[:, u % 2, :], cwb[:, e % 4, :],
                                          ALU.mult).then_inc(s_a, 1)
                    head(nxt, after)
                    if nxt is not None and PART_UNIT <= u < PART_UNIT + 5:
                        parts_step(nxt, u - PART_UNIT)
                y = ring[0][:, :, :].rearrange("p a (c d) -> p (a c) d", d=D)
                dve.wait_ge(s_d, at(b, UNITS, UNITS))
                dve.tensor_tensor(xn2[:, :, :], y, xn2[:, :, :], ALU.add).then_inc(s_y, 1)
                if nxt is not None:
                    for step in HEAD_LEFT:
                        head(nxt, step)

            norm_statistics(0)
            norm_rows(0)
            weights_low(0, slice(0, C_O))
            xt_low(0, ring[1])
            dve.memset(r_s[:, :, :], 0.0).then_inc(s_y, 1)
            weights_low(1, slice(C_O, C_ALL))
            project(0, first=True)
            for n in range(5):
                parts_step(0, n)
            for step in HEAD:
                head(0, step)
            attend(0, 1, None)
            with dve.Fori(0, B - 2) as i:
                ffn(i, i + 1)
                attend(i + 1, i + 2, i)
            ffn(B - 2, B - 1)
            attend(B - 1, None, B - 2)
            ffn(B - 1, None)
            final_statistics(B - 1)
            final_rows(B - 1)

        @block.scalar
        def _(act_e):
            act_e.wait_ge(s_qkvin, 16)
            act_e.activation(w_hi[:, 0:C_O], stage[:, 0:C_O], ACT.Copy).then_inc(s_whi, 1)

            def xt_high(b, slot, first=False):
                act_e.wait_ge(s_xnT, at(b, 1, 1))
                if not first:
                    act_e.wait_ge(s_v, 2 * b)
                act_e.activation(xt_hi[:, :, :], slot[:, :, :], ACT.Copy).then_inc(s_xthi, 1)

            def project(b, first=False):
                if first:
                    act_e.wait_ge(s_pool0, 8)
                else:
                    act_e.wait_ge(s_av, b * N_AV)
                act_e.wait_ge(s_v, at(b, 2, 2))
                v = ring[3][:, :, :].rearrange("p a (c h d) -> p (a c) h d", c=2, h=H)
                for t in range(NT):
                    act_e.activation(v_sb[:, t, :, 0:DH], v[:, t, :, :], ACT.Copy).then_inc(s_vsb, 1)

            def parts_step(b, n, first=False):
                if n == 0 and not first:
                    act_e.wait_ge(s_stack, b * N_STACK * 16)
                if n < 4:
                    act_e.wait_ge(s_sum, at(b, 4, n + 1))
                    act_e.activation(part[:, n // 2, n % 2, 0, :], rot[:, SUM[n], :], ACT.Copy).then_inc(s_phi, 1)
                if n >= 1:
                    m = n - 1
                    act_e.wait_ge(s_pres, at(b, 4, m + 1))
                    act_e.activation(part[:, m // 2, m % 2, 1, :], rot[:, SPARE[m % 2], :], ACT.Copy).then_inc(s_pmid, 1)

            def maxima_rows(b, q):
                act_e.wait_ge(s_mT, at(b, QUADS, q + 1))
                if q:
                    act_e.wait_ge(s_mdma, at(b, 16 * QUADS, 16 * q))
                act_e.activation(mrow[:, :], m_bf[0:12, 0:T], ACT.Copy).then_inc(s_mrow, 1)
                act_e.wait_ge(s_mrow, at(b, QUADS, q + 1))
                act_e.dma_start(q_st[ROWS:MROWS, 4 * q:4 * q + 4, :], mrow[:, :]).then_inc(s_mdma, 16)

            def ht_high(b, k, src, source, high_sem):
                act_e.wait_ge(source, at(b, KD, k + 1))
                act_e.activation(ht_hi[:, k, :], src, ACT.Copy).then_inc(high_sem, 1)

            def load_x(b):
                act_e.wait_ge(s_xnT, b)
                act_e.dma_start(x_ln[:, :, :], x[seq(b)].rearrange("a (t p) d -> p (a t) d", p=P)).then_inc(s_x, 16)

            def attend(b, nxt, prev):
                if nxt is not None:
                    load_x(nxt)
                n = n_st = 0
                for step in PLAN:
                    if step[0] in ("S", "ST"):
                        slot = ring[n % 3]
                        n += 1
                    if step[0] == "ST":
                        _, q, kb, half = step
                        u, width = q * NT + kb, T - kb * P
                        act_e.wait_ge(s_ST, at(b, N_ST, n_st + 1))
                        if u >= 2 and half == 0:
                            act_e.wait_ge(s_av, at(b, N_AV, u - 1))
                        act_e.activation(prob[:, u % 2, 2 * half:2 * half + 2, 0:width], slot[:, :, 0:width],
                                         ACT.Exp, scale=SCALE).then_inc(s_exp, 1)
                        n_st += 1
                    elif step[0] == "MT":
                        maxima_rows(b, step[1])
                    elif step[0] == "AV" and step[2] == NT - 1:
                        q = step[1]
                        act_e.wait_ge(s_av, at(b, N_AV, (q + 1) * NT))
                        if q:
                            act_e.wait_ge(s_oT, at(b, QUADS, q))
                        act_e.activation(o_t[:, :], O_BANK, ACT.Copy).then_inc(s_o, 1)
                    elif step[0] == "AT":
                        ht_high(b, 0, M_BANK, s_aT, s_athi)
                    elif step[0] == "XT" and nxt is not None:
                        xt_high(nxt, ring[1])
                ht_high(b, 1, ring[0][:, 1, :], s_aT, s_athi)

            def ffn(b, nxt):
                for k in range(KD):
                    ht_high(b, k, ring[0][:, k, :], s_hT, s_hthi)
                act_e.wait_ge(s_logit, at(b, 1, 1))
                act_e.activation(sc_t[:, :], ring[0][0:E, 0, :], ACT.Sigmoid).then_inc(s_score, 1)

                def gate_up_high(u):
                    act_e.wait_ge(s_gu, at(b, UNITS, u - 1 if u >= 4 else 1))
                    act_e.activation(gu_hi[:, u % 2, :], expert(u, 0, GU_COLS), ACT.Copy).then_inc(s_guhi, 1)

                def down_high(u):
                    if u >= 4:
                        act_e.wait_ge(s_d, at(b, UNITS, u - 1))
                    act_e.activation(dn_hi[:, u % 2, :], expert(u, GU_COLS, D), ACT.Copy).then_inc(s_dnhi, 1)

                def silu_of(u):
                    act_e.wait_ge(s_gu, at(b, UNITS, u + 1))
                    if u >= 2:
                        act_e.wait_ge(s_t, at(b, UNITS, u - 1))
                    act_e.activation(silu[:, u % 2, :], ring[GU_SLOT[u]][:, 0, :], ACT.Silu).then_inc(s_silu, 1)

                def high(u):
                    if u < SHARED:
                        act_e.wait_ge(s_t, at(b, UNITS, u + 1))
                    else:
                        act_e.wait_ge(s_a, at(b, E, u - SHARED + 1))
                    if u >= 2:
                        act_e.wait_ge(s_d, at(b, UNITS, u - 1))
                    act_e.activation(a_hi[:, u % 2, :], act[:, u % 2, :], ACT.Copy).then_inc(s_ahi, 1)

                act_e.wait_ge(s_wexp, 64)
                for u in range(UNITS + 2):
                    if u == SHARED:
                        act_e.wait_ge(s_cwT, at(b, 1, 1))
                        act_e.activation(cw_t[:, :], ring[3][0:E, 0, :], ACT.Copy).then_inc(s_cwrow, 1)
                    if u < UNITS:
                        silu_of(u)
                    if nxt is not None and ("MT", 0) in head_steps(u - 2):
                        maxima_rows(nxt, 0)
                    if 1 <= u <= UNITS:
                        high(u - 1)
                    if u == 0:
                        gate_up_high(SHARED)
                        gate_up_high(SHARED + 1)
                    elif 4 <= u + 2 < UNITS:
                        gate_up_high(u + 2)
                    if SHARED <= u - 1 < UNITS:
                        down_high(u - 1)
                    if nxt is not None and PART_UNIT <= u < PART_UNIT + 5:
                        parts_step(nxt, u - PART_UNIT)

            xt_high(0, ring[1], first=True)
            act_e.wait_ge(s_small, 16)
            act_e.activation(w_hi[:, C_O:], stage[:, C_O:], ACT.Copy).then_inc(s_whi, 1)
            project(0, first=True)
            for n in range(5):
                parts_step(0, n, first=True)
            maxima_rows(0, 0)
            attend(0, 1, None)
            project(1)
            with act_e.Fori(0, B - 2) as i:
                ffn(i, i + 1)
                attend(i + 1, i + 2, i)
                project(i + 2)
            ffn(B - 2, B - 1)
            attend(B - 1, None, B - 2)
            ffn(B - 1, None)

        @block.tensor
        def _(pe):
            pe.wait_ge(s_pool0, 8)
            pe.wait_ge(s_dve0, 2)

            def split_product(dst, l_hi, l_lo, r_hi, r_lo, start, stop, **kw):
                pe.matmul(dst, l_lo, r_hi, start=start, stop=False, **kw)
                pe.matmul(dst, l_hi, r_lo, start=False, stop=False, **kw)
                return pe.matmul(dst, l_hi, r_hi, start=False, stop=stop, **kw)

            def weight(tile, col, k, width, m, n):
                c = col + k * width + m
                return tile[:, c:c + n]

            def transpose_rows(slot, rows):
                for k in range(KD):
                    for t in range(NT):
                        last = pe.transpose(slot[:, k, t * P:(t + 1) * P], rows[:, t, k * P:(k + 1) * P], ident[:, :])
                return last

            def attention_rows(dst, k):
                for t in range(NT):
                    last = pe.transpose(dst[:, t * P:(t + 1) * P], att[:, t, k * P:(k + 1) * P], ident[:, :])
                last.then_inc(s_aT, 1)

            def xt(b, slot):
                pe.wait_ge(s_xn, at(b, NT, NT))
                transpose_rows(slot, xn).then_inc(s_xnT, 1)

            def qk_products(b, qk):
                pe.wait_ge(s_xtlo, at(b, 1, 1))
                for eo in range(2):
                    m = (2 * qk + eo) * P
                    for k in range(KD):
                        last = split_product(ring[1 + qk][:, eo, :],
                                             weight(w_hi, C_QKV, k, 3 * D, m, P), weight(w_lo, C_QKV, k, 3 * D, m, P),
                                             xt_hi[:, k, :], xt_lo[:, k, :], k == 0, k == KD - 1)
                last.then_inc(s_qk, 1)

            def token_product(slot, lhs_hi, lhs_lo, col, width, m, done):
                for t in range(NT):
                    tok = slice(t * P, (t + 1) * P)
                    for k in range(KD):
                        last = split_product(slot[:, t // 2, (t % 2) * D:(t % 2 + 1) * D],
                                             lhs_hi[:, k, tok], lhs_lo[:, k, tok], weight(w_hi, col, k, width, m, D),
                                             weight(w_lo, col, k, width, m, D), k == 0, k == KD - 1)
                    if t % HT == HT - 1:
                        last.then_inc(done, 1)

            def v_products(b):
                token_product(ring[3], xt_hi, xt_lo, C_QKV, 3 * D, 2 * D, s_v)

            def score_unit(b, n_s, slot):
                pair, qb = S_UNITS[n_s]
                width, q0 = (qb + 1) * P, qb * P
                for j in range(2):
                    h = 2 * pair + j
                    pe.matmul(slot[:, j, 0:width], q_st[0:ROWS, h, q0:q0 + P], k_st[0:ROWS, h, 0:width],
                              start=True, stop=False)
                    last = pe.matmul(slot[:, j, q0:q0 + P], ident_b[:, :], mask_b[:, :], start=False, stop=True)
                last.then_inc(s_S, 1)

            def maxima_unit(b, q):
                pe.wait_ge(s_mp, at(b, 5 * QUADS, 5 * (q + 1)))
                for qb in range(NT):
                    last = pe.transpose(m_bf[0:12, qb * P:(qb + 1) * P],
                                        mpart[:, qb, :, :].rearrange("p s h -> p (s h)"), ident_b[:, :])
                last.then_inc(s_mT, 1)

            def head(b, step, in_ffn=True):
                if step is None:
                    return
                i = HEAD.index(step)
                slot = HEAD_SLOT[i]
                before = last_head(slot, i)
                if i == 0:
                    pe.wait_ge(s_stack, at(b, N_STACK * 16, N_STACK * 16))
                if before is not None:
                    if HEAD[before][0] == "MT":
                        pe.wait_ge(s_mrow, at(b, QUADS, 1))
                    else:
                        pe.wait_ge(s_max, at(b, N_S, HEAD[before][1] + 1))
                elif in_ffn:
                    last_gu = max(u for u in range(UNITS) if GU_SLOT[u] == slot)
                    pe.wait_ge(s_t, at(b - 1, UNITS, last_gu + 1))
                elif slot == 3:
                    pe.wait_ge(s_vsb, at(b, NT, NT))
                if step[0] == "MT":
                    maxima_unit(b, step[1])
                else:
                    score_unit(b, step[1], ring[slot])

            def attend(b, nxt, prev):
                n = n_st = 0
                user = [None] * 3
                user[0] = (s_y, at(b, 1, 1))
                user[1] = (s_max, at(b, N_S, HEAD[last_head(1)][1] + 1))
                user[2] = (s_max, at(b, N_S, HEAD[last_head(2)][1] + 1))
                m_user = (s_max, at(b, N_S, HEAD[last_head(3)][1] + 1))
                o_user = m_user

                for step in PLAN:
                    kind = step[0]
                    if kind in ("S", "ST"):
                        r = n % 3
                        slot = ring[r]
                        n += 1
                        if user[r] is not None:
                            pe.wait_ge(*user[r])
                    if kind == "S":
                        score_unit(b, step[1], slot)
                        user[r] = (s_max, at(b, N_S, step[1] + 1))
                    elif kind == "ST":
                        _, q, kb, half = step
                        if kb == 0 and half == 0:
                            pe.wait_ge(s_mdma, at(b, 16 * QUADS, 16 * (q + 1)))
                        for j in range(2):
                            h = 4 * q + 2 * half + j
                            last = pe.matmul(slot[:, j, 0:T - kb * P], k_st[0:MROWS, h, kb * P:(kb + 1) * P],
                                             q_st[0:MROWS, h, kb * P:T], start=True, stop=True)
                        last.then_inc(s_ST, 1)
                        n_st += 1
                        user[r] = (s_exp, at(b, N_ST, n_st))
                    elif kind == "AV":
                        _, q, kb = step
                        u = q * NT + kb
                        pe.wait_ge(s_tri, at(b, 2 * N_AV, 2 * (u + 1)))
                        if kb == 0:
                            if u == 0:
                                pe.wait_ge(*o_user)
                                pe.wait_ge(s_vsb, at(b, NT, NT))
                            else:
                                pe.wait_ge(s_o, at(b, QUADS, q))
                        for j in range(4):
                            last = pe.matmul(O_BANK[32 * j:32 * j + 32, kb * P:T], v_sb[:, kb, 4 * q + j, :],
                                             prob[:, u % 2, j, 0:T - kb * P], start=(kb == 0), stop=(kb == NT - 1))
                        last.then_inc(s_av, 1)
                    elif kind == "MT":
                        q = step[1]
                        pe.wait_ge(*m_user)
                        maxima_unit(b, q)
                        m_user = (s_mrow, at(b, QUADS, q + 1))
                    elif kind == "OT":
                        q = step[1]
                        pe.wait_ge(s_o, at(b, QUADS, q + 1))
                        pe.wait_ge(*m_user)
                        for t in range(NT):
                            last = pe.transpose(M_BANK[:, t * P:(t + 1) * P], o_t[:, t * P:(t + 1) * P], ident[:, :])
                        last.then_inc(s_oT, 1)
                        m_user = (s_att, at(b, QUADS, q + 1))
                    elif kind == "AT":
                        pe.wait_ge(s_att, at(b, QUADS, 2))
                        pe.wait_ge(*m_user)
                        attention_rows(M_BANK, 0)
                        m_user = (s_atlo, at(b, KD, 1))
                    elif kind == "XT" and nxt is not None:
                        pe.wait_ge(*user[1])
                        xt(nxt, ring[1])
                pe.wait_ge(s_att, at(b, QUADS, QUADS))
                pe.wait_ge(*user[0])
                attention_rows(ring[0][:, 1, :], 1)
                if nxt is not None:
                    qk_products(nxt, 0)
                pe.wait_ge(s_atlo, at(b, KD, KD))
                token_product(ring[0], ht_hi, ht_lo, C_O, D, 0, s_op)
                if nxt is not None:
                    qk_products(nxt, 1)
                    v_products(nxt)

            def ffn(b, nxt):
                for h in range(2):
                    pe.wait_ge(s_xn2, at(b, NT, (h + 1) * HT))
                    for k in range(KD):
                        for t in HALVES[h]:
                            last = pe.transpose(ring[0][:, k, t * P:(t + 1) * P], xn2[:, t, k * P:(k + 1) * P],
                                                ident[:, :])
                        if h == 1:
                            last.then_inc(s_hT, 1)
                pe.wait_ge(s_htlo, at(b, KD, KD))
                for k in range(KD):
                    g_hi, g_lo = weight(w_hi, C_GATE, k, E, 0, E), weight(w_lo, C_GATE, k, E, 0, E)
                    pe.matmul(ring[0][0:E, 0, :], g_lo, ht_lo[:, k, :], start=(k == 0), stop=False)
                    last = split_product(ring[0][0:E, 0, :], g_hi, g_lo, ht_hi[:, k, :], ht_lo[:, k, :],
                                         False, k == KD - 1)
                last.then_inc(s_logit, 1)

                def scores_to_tokens():
                    pe.wait_ge(s_score, at(b, 1, 1))
                    for t in range(NT):
                        last = pe.matmul(ring[0][:, 1, t * E:(t + 1) * E], sc_t[:, t * P:(t + 1) * P],
                                         ident[0:E, 0:E], start=True, stop=True)
                    last.then_inc(s_scT, 1)

                def gate_up(u):
                    if u == 0 and nxt is not None:
                        pe.wait_ge(s_vsb, at(nxt, NT, NT))
                    if u in (1, 2) and nxt is not None:
                        pe.wait_ge(s_rot, at(nxt, 8, 4 * u))
                    if u == 3:
                        pe.wait_ge(s_cwrow, at(b, 1, 1))
                    if u >= 3:
                        before = max(v for v in range(u) if GU_SLOT[v] == GU_SLOT[u])
                        pe.wait_ge(s_t, at(b, UNITS, before + 1))
                    if u >= SHARED:
                        pe.wait_ge(s_gulo, at(b, E, u - SHARED + 1))
                    for n in range(2):
                        if u == 0 and n == 1:
                            scores_to_tokens()
                        for k in range(KD):
                            if u < SHARED:
                                c = (C_SG, C_SU)[n]
                                hi, lo = weight(w_hi, c, k, D, u * P, P), weight(w_lo, c, k, D, u * P, P)
                            else:
                                c = (n * KD + k) * FI
                                hi, lo = gu_hi[:, u % 2, c:c + FI], gu_lo[:, u % 2, c:c + FI]
                            last = split_product(ring[GU_SLOT[u]][:, n, :], hi, lo, ht_hi[:, k, :], ht_lo[:, k, :],
                                                 k == 0, k == KD - 1)
                    last.then_inc(s_gu, 1)

                def down(u):
                    if u == 0:
                        pe.wait_ge(s_route, at(b, ROUTE_STEPS, 1))
                    pe.wait_ge(s_alo, at(b, UNITS, u + 1))
                    if u < SHARED:
                        hi, lo = weight(w_hi, C_SD, u, D, 0, D), weight(w_lo, C_SD, u, D, 0, D)
                    else:
                        pe.wait_ge(s_dnlo, at(b, E, u - SHARED + 1))
                        hi, lo = dn_hi[:, u % 2, :], dn_lo[:, u % 2, :]
                    for t in range(NT):
                        tok = slice(t * P, (t + 1) * P)
                        last = split_product(ring[0][:, t // 2, (t % 2) * D:(t % 2 + 1) * D],
                                             a_hi[:, u % 2, tok], a_lo[:, u % 2, tok], hi, lo,
                                             u == 0 and t % 2 == 0, u == UNITS - 1, skip_group_check=True)
                    last.then_inc(s_d, 1)

                gate_up(0)
                gate_up(1)
                for u in range(UNITS):
                    if u + 2 < UNITS:
                        gate_up(u + 2)
                    if u == 0:
                        pe.wait_ge(s_cw, at(b, 1, 1))
                        pe.wait_ge(s_t, at(b, UNITS, 1))
                        for t in range(NT):
                            last = pe.transpose(ring[3][0:E, 0, t * P:(t + 1) * P], cw[:, t, :], ident[:, :])
                        last.then_inc(s_cwT, 1)
                    before, after = head_steps(u) if nxt is not None else (None, None)
                    head(nxt, before)
                    down(u)
                    head(nxt, after)
                if nxt is not None:
                    for step in HEAD_LEFT:
                        head(nxt, step)

            xt(0, ring[1])
            pe.wait_ge(s_wlo, 1)
            qk_products(0, 0)
            qk_products(0, 1)
            v_products(0)
            pe.wait_ge(s_wlo, 2)
            for step in HEAD:
                head(0, step, in_ffn=False)
            attend(0, 1, None)
            with pe.Fori(0, B - 2) as i:
                ffn(i, i + 1)
                attend(i + 1, i + 2, i)
            ffn(B - 2, B - 1)
            attend(B - 1, None, B - 2)
            ffn(B - 1, None)


N_STAT = 2 * NT + 1
LN_STEPS = 6 * NT
HT = NT // 2
HALVES = (range(0, HT), range(HT, NT))
ROUTE_STEPS = 31
FLN = 3 * NT


def pack_small(w_q, w_k, w_v, w_o, gate_w, ws_g, ws_u, ws_d):
    def halves(w):
        pairs = w.reshape(H, HALF, 2, D)
        return [pairs[:, :, 0].reshape(P, D).T, pairs[:, :, 1].reshape(P, D).T]

    def tiles(wt):
        return [wt[k * P:(k + 1) * P] for k in range(KD)]

    qkv = np.concatenate(halves(w_q) + halves(w_k) + [w_v.T], axis=1)
    cols = []
    for wt in (qkv, w_o.T, ws_g.T, ws_u.T, ws_d.T, gate_w.T):
        cols += tiles(wt)
    return np.ascontiguousarray(np.concatenate(cols, axis=1))


def pack_experts(wg, wu, wd):
    cols = []
    for e in range(E):
        for w in (wg[e].T, wu[e].T):
            cols += [w[k * P:(k + 1) * P] for k in range(KD)]
        cols.append(wd[e].T)
    return np.ascontiguousarray(np.concatenate(cols, axis=1))


def rope_tables():
    inv = (np.float32(10000.0) ** (np.float32(-2.0) * np.arange(HALF, dtype=np.float32) / np.float32(DH))).astype(np.float32)
    ang = np.arange(T, dtype=np.float32)[None, :] * np.tile(inv, H)[:, None]
    return np.ascontiguousarray(np.stack([np.cos(ang), np.sin(ang)], axis=1).astype(np.float32))


def tie_tables():
    row = (np.arange(NG)[None, :] < np.arange(NG)[:, None]).astype(np.float32).reshape(-1)
    return np.ascontiguousarray(np.broadcast_to(row, (P, row.size)))


def kernel(L0_attn_x, L0_attn_W_q, L0_attn_W_k, L0_attn_W_v, L0_attn_W_o, L0_ffn_gate_w, L0_ffn_gate_bias,
           L0_ffn_Wg, L0_ffn_Wu, L0_ffn_Wd, L0_ffn_Ws_g, L0_ffn_Ws_u, L0_ffn_Ws_d):
    import concourse.bacc as bacc
    from concourse.bass_utils import run_bass_kernel_spmd

    a = np.asarray
    arrays = {
        "x": np.ascontiguousarray(a(L0_attn_x)),
        "w_small": pack_small(a(L0_attn_W_q), a(L0_attn_W_k), a(L0_attn_W_v), a(L0_attn_W_o), a(L0_ffn_gate_w),
                              a(L0_ffn_Ws_g), a(L0_ffn_Ws_u), a(L0_ffn_Ws_d)),
        "w_exp": pack_experts(a(L0_ffn_Wg), a(L0_ffn_Wu), a(L0_ffn_Wd)),
        "rope": rope_tables(),
        "ties": tie_tables(),
        "bias": np.ascontiguousarray(np.broadcast_to(a(L0_ffn_gate_bias), (P, NT, E)).reshape(P, NT * E)),
    }
    nc = bacc.Bacc("TRN2", target_bir_lowering=False, num_devices=1)
    ins = [nc.dram_tensor(n, v.shape, mybir.dt.from_np(v.dtype), kind="ExternalInput").ap() for n, v in arrays.items()]
    out = nc.dram_tensor("out", (B, T, D), mybir.dt.float32, kind="ExternalOutput").ap()
    block_kernel(nc, *ins, out)
    r = run_bass_kernel_spmd(nc, [arrays], core_ids=[0])
    return r.results[0]["out"]
```
